# Optimizing a Trainium2 kernel written in Bass

```python
import numpy as np
import jax
import jax.numpy as jnp

def _softmax(x, axis=-1):
    return jax.nn.softmax(x, axis=axis)

def _gelu(x):
    return jax.nn.gelu(x, approximate=True)

def _silu(x):
    return jax.nn.silu(x)

def _sigmoid(x):
    return jax.nn.sigmoid(x)

def _layernorm(x, axis=-1, eps=1e-05):
    m = jnp.mean(x, axis=axis, keepdims=True)
    v = jnp.var(x, axis=axis, keepdims=True)
    return (x - m) / jnp.sqrt(v + eps)

def _scatter_add(tgt, idx, src, axis=0):
    return tgt.at[idx].add(src)

def _segment_sum(src, seg, n):
    return jax.ops.segment_sum(src, seg, n)
kernel_name = 'mk_gnn_preln_d4_gnn_r64_d43993'

def setup_inputs(seed: int=0):
    np.random.seed(seed)
    _w = jnp.asarray

    def _rec_inputs():
        import jax
        import jax.numpy as jnp
        _gk = jax.random.key(seed)
        x = -0.000202 + 1 * jax.random.normal(jax.random.fold_in(_gk, 1), (100000, 64), jnp.float32)
        src = jax.random.randint(jax.random.fold_in(_gk, 2), (50000,), 0, 100000, jnp.int32)
        dst = jnp.minimum((100000 * jax.random.uniform(jax.random.fold_in(_gk, 3), (50000,)) ** 2.0).astype(jnp.int32), 99999)
        _o = jnp.argsort(dst, stable=True)
        src = src[_o]
        dst = dst[_o]
        edge_attr_64 = -6.74381e-05 + 0.999835 * jax.random.normal(jax.random.fold_in(_gk, 12), (50000, 64), jnp.float32)
        edge_weight = jax.random.uniform(jax.random.fold_in(_gk, 13), (50000,), jnp.float32, 0.0, 1)
        edge_weight1 = jax.random.uniform(jax.random.fold_in(_gk, 14), (50000, 1), jnp.float32, 0.0, 1)
        return (x, src, dst, edge_attr_64, edge_weight, edge_weight1)
    x, src, dst, edge_attr_64, edge_weight, edge_weight1 = _rec_inputs()

    def _L0_gnn_setup():
        import jax, jax.numpy as jnp
        import numpy as np
        N_NODES = 100000
        N_EDGES = 25000
        D_FEAT = 64
        key = jax.random.key(seed)
        k_x, k_src, k_dst, k_w = jax.random.split(key, 4)
        x = jax.random.normal(k_x, (N_NODES, D_FEAT), dtype=jnp.float32)
        src = jax.random.randint(k_src, (N_EDGES,), 0, N_NODES, dtype=jnp.int64)
        dst = jax.random.randint(k_dst, (N_EDGES,), 0, N_NODES, dtype=jnp.int64)
        w = jax.random.uniform(k_w, (N_EDGES,), dtype=jnp.float32)
        return {'x': x, 'src': src, 'dst': dst, 'w': w}
    _L0_gnn_all = _L0_gnn_setup()
    _L0_gnn_in = {k: v for k, v in _L0_gnn_all.items() if k in ()}
    del _L0_gnn_all

    def _L1_gnn_setup():
        import jax, jax.numpy as jnp
        import numpy as np
        N_ATOMS = 100000
        N_EDGES = 1250000
        N_FEAT = 64
        key = jax.random.key(seed)
        k1, k2, k3, k4 = jax.random.split(key, 4)
        x = jax.random.normal(k1, (N_ATOMS, N_FEAT), dtype=jnp.float32)
        Wij = jax.random.normal(k2, (N_EDGES, N_FEAT), dtype=jnp.float32)
        idx_i = jnp.sort(jax.random.randint(k3, (N_EDGES,), 0, N_ATOMS, dtype=jnp.int32))
        idx_j = jax.random.randint(k4, (N_EDGES,), 0, N_ATOMS, dtype=jnp.int32)
        return {'x': x, 'Wij': Wij, 'idx_i': idx_i, 'idx_j': idx_j}
    _L1_gnn_all = _L1_gnn_setup()
    _L1_gnn_in = {k: v for k, v in _L1_gnn_all.items() if k in ()}
    del _L1_gnn_all

    def _L2_gnn_setup():
        import jax, jax.numpy as jnp
        import numpy as np
        N_NODES = 50000
        N_EDGES = 12500
        IN_DIM = 64
        OUT_DIM = 64
        NEG_SLOPE = 0.01

        def _forward(v, pre_w, Wa, att_w, Wg, gate_w, src, dst):
            N = v.shape[0]
            z = v @ Wa
            z_src = z[src]
            z_dst = z[dst]
            e = jnp.concatenate([pre_w * z_src, z_dst], axis=1) @ att_w
            e = jax.nn.leaky_relu(e, NEG_SLOPE)[:, 0]
            e_max = jax.ops.segment_max(e, dst, num_segments=N)
            e_max = jnp.where(jnp.isfinite(e_max), e_max, 0.0)
            ex = jnp.exp(e - e_max[dst])
            denom = jax.ops.segment_sum(ex, dst, num_segments=N)
            alpha = ex / jnp.maximum(denom[dst], 1e-30)
            h = jax.ops.segment_sum(alpha[:, None] * z_src, dst, num_segments=N)
            pw = pre_w * v[src]
            gate_proj = pw @ Wg
            deg = jax.ops.segment_sum(jnp.ones((src.shape[0],), v.dtype), dst, num_segments=N)
            max_feat = jax.ops.segment_max(gate_proj, dst, num_segments=N)
            max_feat = jnp.where(deg[:, None] > 0, max_feat, 0.0)
            mean_feat = jax.ops.segment_sum(pw, dst, num_segments=N) / jnp.maximum(deg, 1.0)[:, None]
            g_comb = jnp.concatenate([v, max_feat, mean_feat], axis=1)
            g_val = jax.nn.sigmoid(g_comb @ gate_w)
            return g_val * h
        key = jax.random.key(seed)
        ks = jax.random.split(key, 8)
        gain = np.sqrt(2.0)

        def xavier(k, shape):
            fan_in, fan_out = (shape[0], shape[1])
            std = gain * np.sqrt(2.0 / (fan_in + fan_out))
            return jax.random.normal(k, shape, dtype=jnp.float32) * std
        return {'v': jax.random.normal(ks[0], (N_NODES, IN_DIM), dtype=jnp.float32), 'pre_w': jax.random.uniform(ks[1], (N_EDGES, 1), dtype=jnp.float32), 'Wa': xavier(ks[2], (IN_DIM, OUT_DIM)), 'att_w': xavier(ks[3], (2 * OUT_DIM, 1)), 'Wg': xavier(ks[4], (IN_DIM, OUT_DIM)), 'gate_w': xavier(ks[5], (2 * IN_DIM + OUT_DIM, 1)), 'src': jax.random.randint(ks[6], (N_EDGES,), 0, N_NODES, dtype=jnp.int32), 'dst': jax.random.randint(ks[7], (N_EDGES,), 0, N_NODES, dtype=jnp.int32)}
    _L2_gnn_all = _L2_gnn_setup()
    _L2_gnn_in = {k: v for k, v in _L2_gnn_all.items() if k in ('Wa', 'att_w', 'Wg', 'gate_w')}
    del _L2_gnn_all

    def _L3_gnn_setup():
        import jax, jax.numpy as jnp
        import numpy as np
        N_NODES = 100000
        N_EDGES = 25000
        D_FEAT = 64
        key = jax.random.key(seed)
        k1, k2, k3 = jax.random.split(key, 3)
        features = jax.random.normal(k1, (N_NODES, D_FEAT), dtype=jnp.float32)
        row = jax.random.randint(k2, (N_EDGES,), 0, N_NODES, dtype=jnp.int64 if jax.config.jax_enable_x64 else jnp.int32)
        col = jax.random.randint(k3, (N_EDGES,), 0, N_NODES, dtype=jnp.int64 if jax.config.jax_enable_x64 else jnp.int32)
        return {'features': features, 'row': row, 'col': col}
    _L3_gnn_all = _L3_gnn_setup()
    _L3_gnn_in = {k: v for k, v in _L3_gnn_all.items() if k in ()}
    del _L3_gnn_all
    return {'x': x, 'src': src, 'dst': dst, 'edge_attr_64': edge_attr_64, 'edge_weight': edge_weight, 'edge_weight1': edge_weight1, 'L2_gnn_Wa': _L2_gnn_in['Wa'], 'L2_gnn_att_w': _L2_gnn_in['att_w'], 'L2_gnn_Wg': _L2_gnn_in['Wg'], 'L2_gnn_gate_w': _L2_gnn_in['gate_w']}

def reference(x, src, dst, edge_attr_64, edge_weight, edge_weight1, L2_gnn_Wa, L2_gnn_att_w, L2_gnn_Wg, L2_gnn_gate_w):
    import jax
    import jax.numpy as jnp

    def _L0_gnn_ref(x, src, dst, w):
        import jax, jax.numpy as jnp
        import numpy as np
        N_NODES = 100000
        N_EDGES = 25000
        D_FEAT = 64
        msgs = x[src] * w[:, None]
        out = jax.ops.segment_sum(msgs, dst, num_segments=N_NODES)
        return out

    def _L1_gnn_ref(x, Wij, idx_i, idx_j):
        import jax, jax.numpy as jnp
        import numpy as np
        N_ATOMS = 100000
        N_EDGES = 1250000
        N_FEAT = 64
        x_ij = x[idx_j] * Wij
        y = jax.ops.segment_sum(x_ij, idx_i, num_segments=x.shape[0])
        return y

    def _L2_gnn_ref(v, pre_w, Wa, att_w, Wg, gate_w, src, dst):
        import jax, jax.numpy as jnp
        import numpy as np
        N_NODES = 50000
        N_EDGES = 12500
        IN_DIM = 64
        OUT_DIM = 64
        NEG_SLOPE = 0.01

        def _forward(v, pre_w, Wa, att_w, Wg, gate_w, src, dst):
            N = v.shape[0]
            z = v @ Wa
            z_src = z[src]
            z_dst = z[dst]
            e = jnp.concatenate([pre_w * z_src, z_dst], axis=1) @ att_w
            e = jax.nn.leaky_relu(e, NEG_SLOPE)[:, 0]
            e_max = jax.ops.segment_max(e, dst, num_segments=N)
            e_max = jnp.where(jnp.isfinite(e_max), e_max, 0.0)
            ex = jnp.exp(e - e_max[dst])
            denom = jax.ops.segment_sum(ex, dst, num_segments=N)
            alpha = ex / jnp.maximum(denom[dst], 1e-30)
            h = jax.ops.segment_sum(alpha[:, None] * z_src, dst, num_segments=N)
            pw = pre_w * v[src]
            gate_proj = pw @ Wg
            deg = jax.ops.segment_sum(jnp.ones((src.shape[0],), v.dtype), dst, num_segments=N)
            max_feat = jax.ops.segment_max(gate_proj, dst, num_segments=N)
            max_feat = jnp.where(deg[:, None] > 0, max_feat, 0.0)
            mean_feat = jax.ops.segment_sum(pw, dst, num_segments=N) / jnp.maximum(deg, 1.0)[:, None]
            g_comb = jnp.concatenate([v, max_feat, mean_feat], axis=1)
            g_val = jax.nn.sigmoid(g_comb @ gate_w)
            return g_val * h
        return _forward(v, pre_w, Wa, att_w, Wg, gate_w, src, dst)

    def _L3_gnn_ref(features, row, col):
        import jax, jax.numpy as jnp
        import numpy as np
        N_NODES = 100000
        N_EDGES = 25000
        D_FEAT = 64
        n = features.shape[0]
        gathered = features[col]
        summed = jax.ops.segment_sum(gathered, row, num_segments=n)
        ones = jnp.ones((row.shape[0],), dtype=features.dtype)
        deg = jax.ops.segment_sum(ones, row, num_segments=n)
        deg = jnp.clip(deg, 1.0, None)
        agg = summed / deg[:, None]
        return features + agg
    h = jnp.maximum(_layernorm(x, axis=-1), 0.0)
    x = x + _L0_gnn_ref(h, src, dst, edge_weight)
    h = jnp.maximum(_layernorm(x, axis=-1), 0.0)
    x = x + _L1_gnn_ref(h, edge_attr_64, src, dst)
    h = jnp.maximum(_layernorm(x, axis=-1), 0.0)
    x = x + _L2_gnn_ref(h, edge_weight1, L2_gnn_Wa, L2_gnn_att_w, L2_gnn_Wg, L2_gnn_gate_w, src, dst)
    h = jnp.maximum(_layernorm(x, axis=-1), 0.0)
    x = x + _L3_gnn_ref(h, src, dst)
    return x

_drawn_inputs = setup_inputs


def setup_inputs(seed=0):
    import zlib

    import numpy as np

    out = dict(_drawn_inputs(seed))
    spreads = {}
    factors = {}
    for name, (base, spread) in spreads.items():
        noise = np.random.default_rng([zlib.crc32(name.encode()), seed]).standard_normal(out[name].shape)
        drawn = base * np.exp(spread * noise) if base else spread * noise
        out[name] = jnp.asarray(drawn.astype(out[name].dtype))
    for name, factor in factors.items():
        out[name] = (out[name] * factor).astype(out[name].dtype)
    return out
```

```python
from contextlib import ExitStack

import concourse.bass as bass
from concourse import mybir

P = 128
D = 64
W = D + 1
K = 14
EPS = 1e-5
BIG = 3.0e38
LOW = -1.0e30
GROUPS = [(0, 4), (4, 4), (8, 4), (12, 2)]
SC = 512
LOWBITS = 14
BIAS = 512
FILL = 130000

F32 = mybir.dt.float32
I32 = mybir.dt.int32
ALU = mybir.AluOpType
ACT = mybir.ActivationFunctionType
AX = mybir.AxisListType.X


class Count:

    def __init__(self):
        self.base, self.n = 0, 0

    def up(self):
        self.n += 1
        return 1

    def now(self):
        return self.base + self.n

    def enter(self, i, first, per):
        self.start, self.per = self.base + self.n, per
        self.base, self.n = (i - first) * per + self.start, 0

    def leave(self, times):
        assert self.n == self.per, f"the body counts {self.n}, not {self.per}"
        self.base, self.n = self.start + self.per * times, 0


def gnn_kernel(nc, x, src, dst, attr, w, w1, Wa, att_w, Wg, gate_w, out):
    N, E = x.shape[0], src.shape[0]
    EQ, ER = divmod(E, P)
    NQ, NR = divmod(N, P)
    PAIRS = -(-(EQ + 1) // (2 * K))
    CHUNKS = 2 * PAIRS
    EC = K * CHUNKS
    TILES = 2 * CHUNKS
    assert PAIRS >= 3 and EC - K < EQ and K * (TILES - 1) < NQ < NQ + 1 <= K * TILES
    assert 32 * EC <= 2 ** LOWBITS and EC <= SC and N < FILL and (FILL + BIAS) << LOWBITS < 0x7F800000
    JUNK = (2 * K + 1) * P
    assert out.shape[0] == N + JUNK

    def runs(view, q, r):
        a = view[0:r * (q + 1), :].rearrange("(p t) d -> p t d", t=q + 1)
        b = view[r * (q + 1):r * (q + 1) + (P - r) * q, :].rearrange("(p t) d -> p t d", t=q)
        return a, b

    with ExitStack() as ctx:
        def sb(name, shape, dt=F32):
            return ctx.enter_context(nc.sbuf_tensor("t_" + name, shape, dt))

        def psum(name, shape):
            return ctx.enter_context(nc.psum_tensor("p_" + name, shape, F32))

        def sem(name):
            return ctx.enter_context(nc.semaphore(name))

        nodes = nc.dram_tensor("nodes", (N + JUNK, D), F32).ap()
        filters = nc.dram_tensor("filters", (P * EC, W), F32).ap()
        sorted_src = nc.dram_tensor("sorted_src", (P * SC, 1), F32).ap()
        sorted_slot = nc.dram_tensor("sorted_slot", (P * SC, 1), F32).ap()

        dst_i = sb("dst_i", [P, EC], I32)
        src_i = sb("src_i", [P, EC], I32)
        wt = sb("w", [P, EC])
        w1t = sb("w1", [P, EC])
        same_d = sb("same_d", [P, EC])
        pick_d = sb("pick_d", [P, EC])
        final_d = sb("final_d", [P, EC], I32)
        slot_s = sb("slot_s", [P, EC], I32)
        cap = slot_s[:, :].bitcast(F32)
        dst_s = sb("dst_s", [P, EC], I32)
        same_s = sb("same_s", [P, EC])
        pick_s = sb("pick_s", [P, EC])
        final_s = sb("final_s", [P, EC], I32)
        real = sb("real", [P, EC])
        rdeg = sb("rdeg", [P, EC])
        score_max = sb("score_max", [P, 1 + EC])
        gate_sum = sb("gate_sum", [P, 1 + EC])
        weight_sum = sb("weight_sum", [P, 1 + EC])

        kept = sb("kept", [P, EC * D])
        stage = sb("stage", [P, 2, K], I32)
        stage_dst = sb("stage_dst", [P, 2, K], I32)
        got = sb("got", [P, 2, K * W])
        outrow = sb("outrow", [P, 2, K * D])
        got_dst = sb("got_dst", [P, 2, K * D])
        rowin = sb("rowin", [P, 4 * K * D])
        mask_rep = sb("mask_rep", [P, 2, D, K + 1])
        msg = sb("msg", [P, 2, D, K + 1])
        run = sb("run", [P, 2, D, K + 1])
        picked = sb("picked", [P, D, K])
        center = sb("center", [P, 2, K * D])
        hrow = sb("hrow", [P, 2, K * D])
        hT = rowin[0:D, :].rearrange("p (s a) -> p s a", s=2)
        filter_in = rowin[:, 0:2 * K * W].rearrange("p (s t w) -> p s t w", s=2, w=W)
        rowsum = sb("rowsum", [P, 2, K])
        negmean = sb("negmean", [P, 2, K])
        stats = sb("stats", [P, 2, K, 6])
        apart = sb("apart", [P, 2, K])
        sumsq = sb("sumsq", [P, 2, K])
        std = sb("std", [P, 2, K])
        rstd = sb("rstd", [P, 2, K])
        score = sb("score", [P, K])
        share = sb("share", [P, K])
        gate_dst = sb("gate_dst", [P, 2, K])
        expo = sb("expo", [P, 2, K])
        wexp = sb("wexp", [P, 2, 2, K])
        decay = sb("decay", [P, 2, K])
        gate = sb("gate", [P, K])
        gexp = sb("gexp", [P, K])
        coef = sb("coef", [P, 2, K])
        shift = sb("shift", [P, 2, K])

        words = msg[:, :, :, :].rearrange("p a f t -> p (a f t)")
        words2 = mask_rep[:, :, :, :].rearrange("p a f t -> p (a f t)")
        key = [words[:, 0:SC], words[:, SC:2 * SC]]
        tag = [words[:, 2 * SC:3 * SC], words2[:, 0:SC]]
        swap = words2[:, SC:SC + SC // 2]
        diff = words2[:, SC + SC // 2:2 * SC]
        half = words2[:, 2 * SC:3 * SC]

        pidx_i = sb("pidx_i", [P, 1], I32)
        pbit_i = sb("pbit_i", [P, 8], I32)
        pidx = sb("pidx", [P, 1])
        pbit = sb("pbit", [P, 8])
        ends_d = sb("ends_d", [P, 2], I32)
        ends_s = sb("ends_s", [P, 2])
        endf = sb("endf", [P, 2])
        cont_d, cont_s = sb("cont_d", [P, 2]), sb("cont_s", [P, 2])
        notn = sb("notn", [P, 1])
        side_final_d = sb("side_final_d", [P, 1], I32)
        side_final_s = sb("side_final_s", [P, 1], I32)
        tmp = sb("tmp", [P, 4])
        eps = sb("eps", [P, 1])
        ident = sb("ident", [P, P])
        wa_sb = sb("wa_sb", [D, D])
        WgWa = sb("WgWa", [D, 2 * D])
        att = sb("att", [D, 2])
        waT = sb("waT", [D, D])
        src_w = sb("src_w", [D, 2])
        dst_w = sb("dst_w", [D, 2])
        gmax_w = sb("gmax_w", [P, D])
        side_sum = sb("side_sum", [P, D])
        side_max = sb("side_max", [P, D])
        side_part = sb("side_part", [P, D])
        side_out = sb("side_out", [P, D])
        side_s = sb("side_s", [P, 24])
        room = hrow[:, :, :].rearrange("p s a -> p (s a)")

        def take(rows, at, n, width):
            return room[0:rows, at:at + n * width].rearrange("p (n w) -> p n w", n=n)

        tails = take(P, 0, 4, W)
        inT = take(W, 4 * W, 4, P)
        room2 = center[:, :, :].rearrange("p s a -> p (s a)")
        chainT = room2[0:W, 0:4 * (P + 1)].rearrange("p (n w) -> p n w", w=P + 1)
        expT = take(W, 4 * W + 4 * P, 2, P)
        wexpT = take(W, 4 * W + 6 * P, 2, P)
        assert 4 * W + 8 * P <= 2 * K * D
        maskT = sb("maskT", [W, 3, P])
        capT = room2[0:W, 4 * (P + 1):4 * (P + 1) + P]
        for_counts = picked[:, :, :].rearrange("p f t -> p (f t)")[:, 0:EC]
        assert D * K >= EC

        hT_ps = psum("hT_ps", [P, 2, 512])
        feat_ps = psum("feat_ps", [P, 1024])
        value_ps = psum("value_ps", [P, 1024])
        share_ps = psum("share_ps", [P, 512])
        side_ps = psum("side_ps", [P, 512])

        src_loaded, loaded, consts = sem("src_loaded"), sem("loaded"), sem("consts")
        src_ready = sem("src_ready")
        dve_step = sem("dve_step")
        masks_set = sem("masks_set")
        ready_d, ready_s = sem("ready_d"), sem("ready_s")
        sort_done, sort_stored, sort_loaded = sem("sort_done"), sem("sort_stored"), sem("sort_loaded")
        nodes_copied, zeroed = sem("nodes_copied"), sem("zeroed")
        filter_loaded = [sem(f"filter_loaded{s}") for s in range(2)]
        filter_stored = [sem(f"filter_stored{s}") for s in range(2)]
        filter_named = sem("filter_named")
        landed = [sem(f"landed{s}") for s in range(2)]
        landed_dst = [sem(f"landed_dst{s}") for s in range(2)]
        scattered = [sem(f"scattered{s}") for s in range(2)]
        side_scattered = sem("side_scattered")
        side_made = sem("side_made")
        staged = sem("staged")
        got_free = sem("got_free")
        got_dst_free = sem("got_dst_free")
        outrow_made, outrow_free = sem("outrow_made"), sem("outrow_free")
        shifted, rows_made = sem("shifted"), sem("rows_made")
        summed, deviated = sem("summed"), sem("deviated")
        mask_made, scanned = sem("mask_made"), sem("scanned")
        sums_kept = sem("sums_kept")
        kept_made = sem("kept_made")
        hrow_made = sem("hrow_made")
        turned, turned_free = sem("turned"), sem("turned_free")
        shares_made, shares_used = sem("shares_made"), sem("shares_used")
        proj_made = sem("proj_made")
        feat_free, value_free = sem("feat_free"), sem("value_free")
        expo_made, exp_done = sem("expo_made"), sem("exp_done")
        decay_made, decay_rep = sem("decay_made"), sem("decay_rep")
        gate_made, gate_exp = sem("gate_made"), sem("gate_exp")
        gate_scanned = sem("gate_scanned")
        side_ready, side_turned = sem("side_ready"), sem("side_turned")
        side_act, side_acted = sem("side_act"), sem("side_acted")
        x_loaded = [sem(f"x_loaded{j}") for j in range(4)]
        x_used, out_made = sem("x_used"), sem("out_made")
        outs_stored = [sem(f"outs_stored{s}") for s in range(2)]
        pool_goes, act_goes, pe_goes = sem("pool_goes"), sem("act_goes"), sem("pe_goes")

        LANDS = 16 * K * PAIRS
        SMALL_LOADS = 3 * 3 + 4 + 8
        STAGE_OF = [1, 2, 4, 5]
        NORMS = [0, CHUNKS, 2 * CHUNKS, 3 * CHUNKS]
        NODE_ROWS = nodes[0:N, :]

        ctx.enter_context(nc.allow_non_contiguous_dma(reason="single numbers of the runs' ends"))
        block = ctx.enter_context(nc.Block())

        def bc_f(ap):
            return ap.unsqueeze(2).to_broadcast([P, K, D])

        def bc_t(ap):
            return ap.unsqueeze(1).to_broadcast([P, D, K])

        def tk(ap):
            return ap.rearrange("p (t f) -> p t f", f=D)

        def by_slot(ap):
            return ap.rearrange("p f t -> p t f")

        def by_feature(ap):
            return ap.rearrange("p t f -> p f t")

        def flat(ap):
            return ap.rearrange("p f t -> p (f t)")

        def cols(i, s):
            return bass.ds(i * (2 * K) + s * K, K)

        def fcols(i, s):
            return bass.ds(i * (2 * K * D) + s * K * D, K * D)

        def got_rows(s):
            return got[:, s, :].rearrange("p (t w) -> p t w", w=W)

        @block.sync
        def _(sp):
            def load_runs(array, dram, signal):
                a, b = runs(dram, EQ, ER)
                sp.dma_start(array[0:ER, 0:EQ + 1], a[:, :, 0]).then_inc(signal, 16)
                sp.dma_start(array[ER:P, 0:EQ], b[:, :, 0]).then_inc(signal, 16)
                sp.dma_start(array[ER:P, EQ:EQ + 1], b[:, EQ - 1:EQ, 0]).then_inc(signal, 16)

            def load_ends(ends, dram, signal):
                a, b = runs(dram, EQ, ER)
                sp.dma_start(ends[1:ER + 1, 0:1], a[:, EQ:EQ + 1, 0]).then_inc(signal, 16)
                sp.dma_start(ends[ER + 1:P, 0:1], b[0:P - ER - 1, EQ - 1:EQ, 0]).then_inc(signal, 16)
                sp.dma_start(ends[0:ER - 1, 1:2], a[1:ER, 0:1, 0]).then_inc(signal, 16)
                sp.dma_start(ends[ER - 1:P - 1, 1:2], b[:, 0:1, 0]).then_inc(signal, 16)

            load_runs(src_i, src, src_loaded)
            for array, dram in ((dst_i, dst), (wt, w), (w1t, w1)):
                load_runs(array, dram, loaded)
            sp.wait_ge(masks_set, 1)
            load_ends(ends_d, dst, loaded)
            sp.dma_start(wa_sb[:, :], Wa).then_inc(loaded, 16)
            sp.dma_start(WgWa[:, 0:D], Wg).then_inc(loaded, 16)
            sp.dma_start(WgWa[:, D:2 * D], Wa).then_inc(loaded, 16)
            for c in range(2):
                sp.dma_start(att[:, c:c + 1], att_w[c * D:(c + 1) * D, :]).then_inc(loaded, 16)
            sp.dma_start(dst_w[:, 1:2], gate_w[0:D, :]).then_inc(loaded, 16)
            sp.dma_start(src_w[:, 1:2], gate_w[2 * D:3 * D, :]).then_inc(loaded, 16)
            sp.dma_start(gmax_w[:, :], gate_w.rearrange("(a d) o -> a (d o)", d=D)[1:2, :].to_broadcast([P, D])).then_inc(loaded, 16)

            def copy_nodes(i, last=False):
                na, nb = (NQ + 1, NQ) if last else (4 * K * PAIRS, 4 * K * PAIRS)
                for a, b, n_ in zip(runs(x, NQ, NR), runs(NODE_ROWS, NQ, NR), (na, nb)):
                    m = min(4 * K, n_ - 4 * K * (PAIRS - 1))
                    sp.dma_start(b[:, bass.ds(i * (4 * K), m), :],
                                 a[:, bass.ds(i * (4 * K), m), :]).then_inc(nodes_copied, 16)

            sp.wait_ge(masks_set, 2)
            zeros = outrow[:, :, :].rearrange("p s a -> p (s a)")
            for table in (nodes, out):
                sp.dma_start(table[N:N + 2 * K * P, :].rearrange("(p t) d -> p (t d)", p=P),
                             zeros).then_inc(zeroed, 16)
                sp.dma_start(table[N + 2 * K * P:N + JUNK, :], zeros[:, 0:D]).then_inc(zeroed, 16)

            fa, fb = runs(attr, EQ, ER)
            filter_rows = filters.rearrange("(p t) w -> p (t w)", t=EC)

            def load_filter(i, s, last=False):
                na, nb = (EQ + 1 - (EC - K), EQ - (EC - K)) if last else (K, K)
                at = i * (2 * K) + s * K
                for v, lo, hi, m in ((fa, 0, ER, na), (fb, ER, P, nb)):
                    sp.dma_start(filter_in[lo:hi, s, 0:m, 0:D], v[:, bass.ds(at, m), :]).then_inc(filter_loaded[s], 16)

            def store_filter(i, s):
                sp.wait_ge(filter_named, i * 2 + (s + 1))
                sp.dma_start(filter_rows[:, bass.ds(i * (2 * K * W) + s * K * W, K * W)],
                             filter_in[:, s, :, :].rearrange("p t w -> p (t w)")).then_inc(filter_stored[s], 16)

            for s in range(2):
                load_filter(0, s)
            def filter_pairs(first, end):
                with sp.Fori(first, end) as i:
                    for s in range(2):
                        store_filter(i - 1, s)
                        sp.wait_ge(filter_stored[s], i * 16)
                        load_filter(i, s)
                    copy_nodes(i)

            copy_nodes(0)
            MID = min(PAIRS // 2 + 1, PAIRS - 1)
            filter_pairs(1, MID)
            sp.wait_ge(sort_done, 1)
            for dram, array in ((sorted_src, key[0]), (sorted_slot, tag[0])):
                sp.dma_start(dram.rearrange("(p t) o -> p (t o)", t=SC), array).then_inc(sort_stored, 16)
            sp.wait_ge(sort_stored, 32)
            load_runs(score_max[:, 1:1 + EC], sorted_src, sort_loaded)
            load_runs(gate_sum[:, 1:1 + EC], sorted_slot, sort_loaded)
            load_ends(ends_s, sorted_src[0:E, :], sort_loaded)
            if MID < PAIRS - 1:
                filter_pairs(MID, PAIRS - 1)
            for s in range(2):
                store_filter(PAIRS - 2, s)
                sp.wait_ge(filter_stored[s], (PAIRS - 1) * 16)
                load_filter(PAIRS - 1, s, last=(s == 1))
            copy_nodes(PAIRS - 1, last=True)
            for s in range(2):
                store_filter(PAIRS - 1, s)

            for s in range(2):
                sp.wait_ge(scattered[s], 3 * LANDS)
            sp.wait_ge(side_scattered, 48)
            xa, xb = runs(NODE_ROWS, NQ, NR)
            oa, ob = runs(out[0:N, :], NQ, NR)

            def tile_io(i, j, views, tile, load, signal, last):
                na, nb = (NQ + 1 - K * (TILES - 1), NQ - K * (TILES - 1)) if last else (K, K)
                at = i * (4 * K) + j * K
                for v, lo, hi, m in ((views[0], 0, NR, na), (views[1], NR, P, nb)):
                    dram, on_chip = v[:, bass.ds(at, m), :], tk(tile)[lo:hi, 0:m, :]
                    if load:
                        sp.dma_start(on_chip, dram).then_inc(signal, 16)
                    else:
                        sp.dma_start(dram, on_chip).then_inc(signal, 16)

            def load_x(i, j, start, last):
                if not start:
                    sp.wait_ge(x_used, i * 4 + (j - 3))
                tile_io(i, j, (xa, xb), rowin[:, j * K * D:(j + 1) * K * D], True, x_loaded[j], last)

            def store_tile(i, j, last=False):
                sp.wait_ge(out_made, i * 4 + (j + 1))
                tile_io(i, j, (oa, ob), outrow[:, j % 2, :], False, outs_stored[j % 2], last)

            def node_tiles(i, start=False, last=False):
                for j in range(4):
                    load_x(i, j, start, last and j == 3)
                    if j == 3:
                        store_tile(i, 0)
                    elif not start:
                        store_tile(i - 1, j + 1)

            node_tiles(0, start=True)
            with sp.Fori(1, PAIRS - 1) as i:
                node_tiles(i)
            node_tiles(PAIRS - 1, last=True)
            for j in (1, 2, 3):
                store_tile(PAIRS - 1, j, last=(j == 3))
            for s in range(2):
                sp.wait_ge(outs_stored[s], 16 * TILES)
                sp.wait_ge(scattered[s], 4 * LANDS)
            sp.wait_ge(side_scattered, 64)

        @block.gpsimd
        def _(pool):
            junk_i = gate_sum[:, 1:1 + EC].bitcast(I32)
            slot_i = weight_sum[:, 1:1 + EC].bitcast(I32)
            nc.gpsimd.iota(pidx_i[:, :], pattern=[[0, 1]], base=0, channel_multiplier=1).then_inc(consts, 1)
            nc.gpsimd.iota(junk_i, pattern=[[0, PAIRS], [P, 2 * K]], base=N, channel_multiplier=1).then_inc(consts, 1)
            nc.gpsimd.iota(slot_i, pattern=[[1, EC]], base=0, channel_multiplier=EC).then_inc(consts, 1)
            nc.gpsimd.memset(ident[:, :], 0.0).then_inc(consts, 1)
            nc.gpsimd.memset(real[:, 0:EQ + 1], 1.0).then_inc(consts, 1)
            nc.gpsimd.memset(real[:, EQ + 1:EC], 0.0).then_inc(consts, 1)
            pool.wait_ge(consts, 6)
            nc.gpsimd.affine_select(out=ident[:, :], in_=ident[:, :], compare_op=ALU.not_equal, fill=1.0,
                                    base=0, pattern=[[-1, P]], channel_multiplier=1).then_inc(consts, 1)
            nc.gpsimd.affine_select(out=real[:, EQ:EQ + 1], in_=real[:, EQ:EQ + 1], compare_op=ALU.is_ge,
                                    fill=0.0, base=ER - 1, pattern=[[0, 1]],
                                    channel_multiplier=-1).then_inc(consts, 1)
            copies = Count()

            def stage_copy(to, array, i, s):
                nc.gpsimd.tensor_copy(to[:, s, :], array[:, cols(i, s)]).then_inc(staged, copies.up())

            def chunk(i, s, free_at, streams, then=None):
                pool.wait_ge(got_free, i * 2 + (free_at + s + 1))
                if len(streams) == 2:
                    pool.wait_ge(got_dst_free, i * 2 + (s + 1))
                pool.wait_ge(staged, copies.now())
                pool.sem_inc(pool_goes, 1)
                for t in range(K):
                    if t == K // 2 and then:
                        then()
                    for to, from_, width, indices, _, signal in streams:
                        nc.gpsimd.indirect_dma_start(
                            out=to[:, s, t * width:(t + 1) * width], out_offset=None, in_=from_,
                            in_offset=bass.IndirectOffsetOnAxis(ap=indices[:, s, t:t + 1], axis=0),
                        ).then_inc(signal[s], 16)

            def gather_pass(n, free_at, streams):
                def restage(i, s):
                    for k, (_, _, _, indices, array, signal) in enumerate(streams):
                        pool.wait_ge(signal[s], i * (16 * K) + (0 if k else n * LANDS))
                        stage_copy(indices, array, i, s)

                for s in range(2):
                    for k, (_, _, _, indices, array, signal) in enumerate(streams):
                        if n and not k:
                            pool.wait_ge(signal[s], n * LANDS)
                            pool.wait_ge(scattered[s], SCATTERED[n])
                        stage_copy(indices, array, 0, s)
                chunk(0, 0, free_at, streams)
                with pool.Fori(0, PAIRS - 1) as i:
                    copies.enter(i, 0, 2 * len(streams))
                    chunk(i, 1, free_at, streams, lambda: restage(i + 1, 0))
                    chunk(i + 1, 0, free_at, streams, lambda: restage(i + 1, 1))
                    copies.leave(PAIRS - 1)
                chunk(PAIRS - 1, 1, free_at, streams)
                for s in range(2):
                    pool.wait_ge(landed[s], (n + 1) * LANDS)
                    if len(streams) == 2:
                        pool.wait_ge(landed_dst[s], LANDS)

            SCATTERED = [0, LANDS, LANDS, 2 * LANDS, 3 * LANDS]

            def scatter_pass(n, array, side, to):
                def restage(i, s):
                    pool.wait_ge(scattered[s], i * (16 * K) + n * LANDS)
                    pool.sem_inc(outrow_free, 1)
                    stage_copy(stage, array, i, s)

                def scatter(i, s, then=None):
                    pool.wait_ge(outrow_made, i * 2 + (n * CHUNKS + s + 1))
                    pool.wait_ge(staged, copies.now())
                    pool.sem_inc(pool_goes, 1)
                    for t in range(K):
                        if t == K // 2 and then:
                            then()
                        nc.gpsimd.indirect_dma_start(
                            out=to, out_offset=bass.IndirectOffsetOnAxis(ap=stage[:, s, t:t + 1], axis=0),
                            in_=outrow[:, s, t * D:(t + 1) * D], in_offset=None,
                            compute_op=ALU.add).then_inc(scattered[s], 16)

                for s in range(2):
                    stage_copy(stage, array, 0, s)
                scatter(0, 0)
                with pool.Fori(0, PAIRS - 1) as i:
                    copies.enter(i, 0, 2)
                    scatter(i, 1, lambda: restage(i + 1, 0))
                    scatter(i + 1, 0, lambda: restage(i + 1, 1))
                    copies.leave(PAIRS - 1)
                scatter(PAIRS - 1, 1)
                pool.wait_ge(side_made, n + 1)
                nc.gpsimd.indirect_dma_start(
                    out=to, out_offset=bass.IndirectOffsetOnAxis(ap=side[:, 0:1], axis=0),
                    in_=side_out[:, :], in_offset=None, compute_op=ALU.add).then_inc(side_scattered, 16)
                for s in range(2):
                    pool.wait_ge(scattered[s], (n + 1) * LANDS)
                pool.wait_ge(side_scattered, 16 * (n + 1))
                pool.sem_inc(outrow_free, 2)

            pool.wait_ge(src_ready, 1)
            gather_pass(0, 0, [(got, x, D, stage, src_i, landed)])
            pool.wait_ge(nodes_copied, 32 * PAIRS)
            pool.wait_ge(zeroed, 64)
            pool.wait_ge(ready_s, 1)
            scatter_pass(0, final_d, side_final_d, nodes)
            for s in range(2):
                pool.wait_ge(filter_stored[s], 16 * PAIRS)
            gather_pass(1, CHUNKS, [(got, filters, W, stage, slot_s, landed)])
            pool.wait_ge(got_free, 2 + 2 * CHUNKS)
            gather_pass(2, 2 * CHUNKS, [(got, NODE_ROWS, D, stage, dst_s, landed)])
            scatter_pass(1, final_s, side_final_s, nodes)
            gather_pass(3, 3 * CHUNKS, [(got, NODE_ROWS, D, stage, src_i, landed),
                                        (got_dst, NODE_ROWS, D, stage_dst, dst_i, landed_dst)])
            scatter_pass(2, final_d, side_final_d, nodes)
            gather_pass(4, 4 * CHUNKS, [(got, NODE_ROWS, D, stage, dst_s, landed)])
            for s in range(2):
                pool.wait_ge(outs_stored[s], 16 * TILES)
            scatter_pass(3, final_s, side_final_s, out)

        @block.scalar
        def _(act):
            def deviation_of(n, s):
                act.wait_ge(summed, n)
                nc.scalar.activation(std[:, s, :], sumsq[:, s, :], ACT.Sqrt, bias=eps[:, 0:1],
                                     scale=1.0 / D).then_inc(deviated, 1)

            act.wait_ge(loaded, 16 * SMALL_LOADS)
            act.wait_ge(ready_d, 1)
            with act.Fori(0, PAIRS) as i:
                for s in range(2):
                    act.wait_ge(filter_loaded[s], i * 32 + 32)
                    nc.scalar.activation(filter_in[:, s, :, D], dst_i[:, cols(i, s)],
                                         ACT.Copy).then_inc(filter_named, 1)
                    act.wait_ge(landed[s], i * (16 * K) + 16 * K)
                    nc.scalar.activation(kept[:, fcols(i, s)], got[:, s, 0:K * D], ACT.Copy).then_inc(got_free, 1)

            def make_mask(array, i, s, n):
                act.wait_ge(scanned, n)
                nc.scalar.activation(mask_rep[:, s, :, 1:K + 1], bc_t(array[:, cols(i, s)]),
                                     ACT.Copy).then_inc(mask_made, 1)

            def keep_sums(layer, i, s):
                act.wait_ge(scanned, i * 2 + (layer * CHUNKS + s + 3))
                nc.scalar.activation(tk(kept[:, fcols(i, s)]), by_slot(run[:, s, :, 1:K + 1]),
                                     ACT.Copy).then_inc(sums_kept, 1)

            def fill_outrow(n, i, s):
                act.wait_ge(outrow_free, i * 2 + (n * CHUNKS + s + 1))
                act.sem_inc(act_goes, 1)
                nc.scalar.activation(outrow[:, s, :], kept[:, fcols(i, s)], ACT.Copy).then_inc(outrow_made, 1)

            for layer, same, ready in ((0, same_d, masks_set), (1, same_s, ready_s)):
                if layer == 0:
                    act.wait_ge(sort_done, 2)
                    act.wait_ge(zeroed, 64)
                else:
                    act.wait_ge(ready_s, 1)
                    with act.Fori(0, PAIRS) as i:
                        for s in range(2):
                            act.wait_ge(landed[s], i * (16 * K) + (LANDS + 16 * K))
                            nc.scalar.activation(dst_s[:, cols(i, s)], got_rows(s)[:, :, D], ACT.Copy)
                            nc.scalar.activation(tk(kept[:, fcols(i, s)]), got_rows(s)[:, :, 0:D],
                                                 ACT.Copy).then_inc(got_free, 1)
                make_mask(same, 0, 0, layer * CHUNKS + 1)

                def chunk_of(i, s, last):
                    if not (last and s == 1):
                        ni, ns = (i, 1) if s == 0 else (i + 1, 0)
                        make_mask(same, ni, ns, i * 2 + (layer * CHUNKS + s + 2))
                    deviation_of(i * 2 + (NORMS[layer] + s + 1), s)
                    keep_sums(layer, i, s)
                    if layer == 0:
                        act.wait_ge(sums_kept, i * 2 + (s + 3))
                        fill_outrow(0, i, s)

                with act.Fori(0, PAIRS - 1) as i:
                    for s in range(2):
                        chunk_of(i, s, False)
                if layer:
                    act.wait_ge(sums_kept, 2 * CHUNKS)
                    for s in range(2):
                        fill_outrow(1, 0, s)
                for s in range(2):
                    chunk_of(PAIRS - 1, s, True)
            act.wait_ge(sums_kept, 2 * CHUNKS + 2)
            with act.Fori(1, PAIRS) as i:
                for s in range(2):
                    fill_outrow(1, i, s)

            def deviations(g):
                act.wait_ge(summed, g + (NORMS[2] + 1))
                nc.scalar.activation(std[:, :, :], sumsq[:, :, :], ACT.Sqrt, bias=eps[:, 0:1],
                                     scale=1.0 / D).then_inc(deviated, 1)

            def keep_turned(g):
                for side in range(2):
                    for q, (t0, nt) in enumerate(GROUPS):
                        act.wait_ge(turned, g * 8 + (4 * side + q + 1))
                        nc.scalar.activation(hT[:, side, t0 * P:(t0 + nt) * P],
                                             hT_ps[0:D, q % 2, 0:nt * P], ACT.Copy).then_inc(turned_free, 1)

            def exps(g, s):
                act.wait_ge(expo_made, g + 1)
                nc.scalar.activation(wexp[:, s, :, :], expo[:, :, :], ACT.Exp).then_inc(exp_done, 1)
                act.wait_ge(decay_made, g + 1)
                act.wait_ge(scanned, g + (2 * CHUNKS + 2))
                nc.scalar.activation(mask_rep[:, 0, :, 1:K + 1], bc_t(decay[:, s, :]),
                                     ACT.Copy).then_inc(decay_rep, 1)

            def gate_features(i, s):
                act.wait_ge(gate_scanned, i * 2 + (s + 1))
                nc.scalar.activation(mask_rep[:, 1, :, 1:K + 1], bc_t(cap[:, cols(i, s)]),
                                     ACT.Copy).then_inc(mask_made, 1)
                act.wait_ge(proj_made, i * 2 + (s + 1))
                for t in range(K):
                    m = nc.scalar.activation(
                        msg[:, 1, :, 1 + t], feat_ps[:, t * D:(t + 1) * D], ACT.Copy,
                        scale=w1t[:, bass.ds(i * (2 * K) + s * K + t, 1)])
                m.then_inc(feat_free, 1)

            def attend(i, s, more, more2):
                g = i * 2 + s
                if more2:
                    deviations(g + 2)
                gate_features(i, s)
                if more:
                    keep_turned(g + 1)
                act.wait_ge(gate_made, g + 1)
                nc.scalar.activation(gexp[:, :], gate[:, :], ACT.Exp, scale=-1.0).then_inc(gate_exp, 1)
                if more:
                    exps(g + 1, 1 - s)

            act.wait_ge(masks_set, 3)
            deviations(0)
            deviations(1)
            keep_turned(0)
            exps(0, 0)
            with act.Fori(0, PAIRS - 1) as i:
                for s in range(2):
                    attend(i, s, True, True)
            act.wait_ge(kept_made, CHUNKS - 2)
            for s in range(2):
                fill_outrow(2, 0, s)
            attend(PAIRS - 1, 0, True, False)
            attend(PAIRS - 1, 1, False, False)
            act.wait_ge(kept_made, CHUNKS)
            act.wait_ge(side_act, 1)
            nc.scalar.activation(wexpT, expT, ACT.Exp).then_inc(side_acted, 1)
            act.wait_ge(side_act, 2)
            nc.scalar.activation(side_s[:, 10:12], side_s[:, 8:10], ACT.Exp).then_inc(side_acted, 1)
            act.wait_ge(side_act, 3)
            nc.scalar.activation(side_s[:, 15:16], side_s[:, 14:15], ACT.Exp, scale=-1.0).then_inc(side_acted, 1)
            with act.Fori(1, PAIRS) as i:
                for s in range(2):
                    fill_outrow(2, i, s)

            act.wait_ge(masks_set, 4)
            make_mask(same_s, 0, 0, 3 * CHUNKS + 1)

            def rows_of(i, j):
                c = STAGE_OF[j] % 2
                act.wait_ge(shifted, i * 4 + (j + 1))
                for t in range(K):
                    at = (j * K + t) * D
                    m = nc.scalar.activation(hrow[:, j % 2, t * D:(t + 1) * D], rowin[:, at:at + D], ACT.Relu,
                                             bias=shift[:, c, t:t + 1], scale=rstd[:, c, t:t + 1])
                m.then_inc(rows_made, 1)

            def mixed(i, last=False):
                for m in range(6):
                    s = m // 3
                    if not (last and m == 5):
                        deviation_of(i * 6 + (NORMS[3] + m + 2), (m + 1) % 2)
                    if m % 3:
                        rows_of(i, 2 * s + m % 3 - 1)
                        continue
                    if not (last and s == 1):
                        ni, ns = (i, 1) if s == 0 else (i + 1, 0)
                        make_mask(same_s, ni, ns, i * 2 + (3 * CHUNKS + s + 2))
                    keep_sums(3, i, s)

            deviation_of(NORMS[3] + 1, 0)
            with act.Fori(0, PAIRS - 1) as i:
                mixed(i)
            mixed(PAIRS - 1, last=True)

        @block.tensor
        def _(pe):
            pe.wait_ge(loaded, 16 * SMALL_LOADS)
            pe.wait_ge(consts, 8)
            nc.tensor.transpose(side_ps[0:D, 0:D], wa_sb[:, :], ident[0:D, 0:D]).then_inc(side_turned, 1)
            pe.wait_ge(side_ready, 1)
            nc.tensor.matmul(side_ps[0:D, 0:2], waT[:, :], att[:, :], start=True, stop=True).then_inc(side_turned, 1)

            def turn_tails(n, counts):
                pe.wait_ge(side_ready, n)
                for c in range(counts):
                    m = nc.tensor.transpose(side_ps[0:W, c * P:(c + 1) * P], tails[:, c, :], ident[:, :])
                m.then_inc(side_turned, 1)

            def turn_back(n, counts):
                pe.wait_ge(side_ready, n)
                for c in range(counts):
                    m = nc.tensor.transpose(side_ps[:, c * P:c * P + W], inT[:, c, :], ident[0:W, 0:W])
                m.then_inc(side_turned, 1)

            for layer in range(2):
                turn_tails(2 + 3 * layer, 2)
                turn_tails(3 + 3 * layer, 1)
                turn_back(4 + 3 * layer, 1)
            turn_tails(8, 2)

            def turn_group(g, side, q):
                t0, nt = GROUPS[q]
                pe.wait_ge(turned_free, g * 8 + (4 * side + q + 1))
                pe.sem_inc(pe_goes, 1)
                rows = tk(hrow[:, side, :])
                for t in range(nt):
                    m = nc.tensor.transpose(hT_ps[0:D, q % 2, t * P:(t + 1) * P], rows[:, t0 + t, :], ident[:, :])
                m.then_inc(turned, 1)

            def shares(g, side, q, weights):
                t0, nt = GROUPS[q]
                pe.wait_ge(turned_free, g * 8 + (4 * side + q + 3))
                for t in range(t0, t0 + nt):
                    at = side * 2 * K + 2 * t
                    m = nc.tensor.matmul(share_ps[:, at:at + 2], hT[:, side, t * P:(t + 1) * P],
                                         weights[:, :], start=True, stop=True)
                if side == 1 and q == 3:
                    m.then_inc(shares_made, 1)

            def heads(g):
                pe.wait_ge(shares_used, g + 1)
                for side, weights in ((0, src_w), (1, dst_w)):
                    pe.wait_ge(hrow_made, g * 2 + (side + 1))
                    for q in range(4):
                        turn_group(g, side, q)
                        if q:
                            shares(g, side, q - 1, weights)
                    shares(g, side, 3, weights)
                pe.wait_ge(feat_free, g + 1)
                pe.wait_ge(value_free, g + 1)
                for t in range(K):
                    for c, to in enumerate((feat_ps, value_ps)):
                        m = nc.tensor.matmul(to[:, t * D:(t + 1) * D], hT[:, 0, t * P:(t + 1) * P],
                                             WgWa[:, c * D:(c + 1) * D], start=True, stop=True)
                m.then_inc(proj_made, 1)

            pe.wait_ge(masks_set, 3)
            with pe.Fori(0, PAIRS) as i:
                for s in range(2):
                    heads(i * 2 + s)
            turn_tails(9, 4)
            turn_back(10, 4)
            turn_tails(11, 2)
            turn_tails(12, 2)
            turn_back(13, 2)

        @block.vector
        def _(dve):
            n = Count()
            V = nc.vector

            def settle():
                dve.wait_ge(dve_step, n.now())

            def op(f, *a, **k):
                dve.wait_ge(dve_step, n.now())
                return f(*a, **k).then_inc(dve_step, n.up())

            V.memset(ends_d[:, :], -1).then_inc(dve_step, n.up())
            V.memset(ends_s[:, :], -1.0).then_inc(dve_step, n.up())
            settle()
            dve.sem_inc(masks_set, 1)
            dve.wait_ge(src_loaded, 48)
            for c in range(EQ + 1, EC):
                op(V.tensor_copy, src_i[:, c:c + 1], src_i[:, c - 1:c])
            settle()
            dve.sem_inc(src_ready, 1)
            dve.sem_inc(got_free, 2)

            V.memset(eps[:, :], EPS).then_inc(dve_step, n.up())
            V.memset(outrow[:, :, :], 0.0).then_inc(dve_step, n.up())
            V.memset(run[:, :, :, :], 0.0).then_inc(dve_step, n.up())
            V.memset(filter_in, 0.0).then_inc(dve_step, n.up())
            for row in (side_sum, side_max):
                V.memset(row[:, :], 0.0).then_inc(dve_step, n.up())
            for array in (score_max, gate_sum, weight_sum):
                V.memset(array[:, 0:1], 0.0).then_inc(dve_step, n.up())
            settle()
            dve.sem_inc(masks_set, 1)
            for s_, free in ((scanned, 2), (sums_kept, 2), (got_dst_free, 2),
                             (outrow_free, 2), (turned_free, 2), (shares_used, 1), (feat_free, 1),
                             (value_free, 1), (gate_scanned, 1)):
                dve.sem_inc(s_, free)

            dve.wait_ge(loaded, 16 * SMALL_LOADS)
            dve.wait_ge(consts, 8)
            for c in range(EQ + 1, EC):
                for array in (dst_i, wt, w1t):
                    op(V.tensor_copy, array[:, c:c + 1], array[:, c - 1:c])
            settle()
            dve.sem_inc(ready_d, 1)
            op(V.tensor_tensor, wt[:, :], wt[:, :], real[:, :], ALU.mult)
            op(V.tensor_copy, pidx[:, :], pidx_i[:, :])
            junk, slot = final_d[:, :].bitcast(F32), final_s[:, :].bitcast(F32)
            junk = rdeg[:, :]
            op(V.tensor_copy, junk, gate_sum[:, 1:1 + EC].bitcast(I32))
            op(V.tensor_copy, tag[0][:, 0:EC], weight_sum[:, 1:1 + EC].bitcast(I32))

            pi, kb = key[0].bitcast(I32), key[1].bitcast(I32)
            for b in range(7):
                op(V.tensor_scalar, pbit_i[:, b:b + 1], pidx_i[:, :], b, None, ALU.logical_shift_right)
            op(V.tensor_scalar, pbit_i[:, 0:7], pbit_i[:, 0:7], 1, None, ALU.bitwise_and)
            op(V.tensor_copy, pbit[:, 0:7], pbit_i[:, 0:7])
            op(V.tensor_scalar, tmp[:, 0:1], pbit[:, 5:6], float(32 * EC), None, ALU.mult)
            op(V.tensor_scalar, tmp[:, 1:2], pbit[:, 6:7], float(64 * EC), None, ALU.mult)
            op(V.tensor_tensor, tmp[:, 0:1], tmp[:, 0:1], tmp[:, 1:2], ALU.add)
            op(V.tensor_scalar, pbit[:, 0:7], pbit[:, 0:7], -2.0, 1.0, ALU.mult, ALU.add)
            op(V.tensor_scalar, tag[1].bitcast(I32)[:, 0:EC], tag[0][:, 0:EC], tmp[:, 0:1], None, ALU.subtract)
            h_i = half.bitcast(I32)
            op(V.memset, h_i[:, EC:SC], FILL + BIAS)
            op(V.memset, tag[1].bitcast(I32)[:, EC:SC], 0)
            op(V.tensor_scalar, key[0][:, 0:EC], src_i[:, :], float(-FILL), None, ALU.add)
            op(V.tensor_tensor, key[0][:, 0:EC], key[0][:, 0:EC], real[:, :], ALU.mult)
            op(V.tensor_scalar, h_i[:, 0:EC], key[0][:, 0:EC], float(FILL + BIAS), None, ALU.add)
            op(V.tensor_scalar, h_i, h_i, LOWBITS, None, ALU.logical_shift_left)
            op(V.tensor_tensor, key[0].bitcast(I32), h_i, tag[1].bitcast(I32), ALU.bitwise_or)

            at = [0]

            def turn_blocks():
                a, b = at[0], 1 - at[0]
                op(V.transpose, key[b], key[a])
                if tagged[0]:
                    op(V.transpose, tag[b], tag[a])
                at[0] = b

            tagged = [False]

            def parts(array, j):
                v = array.rearrange("p (b h l) -> p b h l", h=2, l=1 << j)
                return v[:, :, 0, :], v[:, :, 1, :]

            def exchange(views_a, views_b, tags_a, tags_b):
                (lo, hi), (to_lo, to_hi) = views_a, views_b
                if tagged[0]:
                    (tlo, thi), (to_tlo, to_thi) = tags_a, tags_b
                    m, d = like(swap, lo), like(diff, lo)
                    op(V.tensor_tensor, m, lo, hi, ALU.is_gt)
                    V.tensor_tensor(d, thi, tlo, ALU.subtract).then_inc(dve_step, n.up())
                    op(V.tensor_tensor, d, d, m, ALU.mult)
                    op(V.tensor_tensor, to_tlo, tlo, d, ALU.add)
                    V.tensor_tensor(to_thi, thi, d, ALU.subtract).then_inc(dve_step, n.up())
                else:
                    settle()
                V.tensor_tensor(to_lo, lo, hi, ALU.min).then_inc(dve_step, n.up())
                V.tensor_tensor(to_hi, lo, hi, ALU.max).then_inc(dve_step, n.up())

            def like(array, view):
                shape = view.shape
                if len(shape) == 3:
                    return array.rearrange("p (b l) -> p b l", l=shape[2])
                return array

            def column_stage(j):
                a, b = at[0], 1 - at[0]
                exchange(parts(key[a], j), parts(key[b], j), parts(tag[a], j), parts(tag[b], j))
                at[0] = b

            def flip(bit):
                k_ = key[at[0]]
                if bit < 9:
                    hi = parts(k_, bit)[1]
                    op(V.tensor_scalar, hi, hi, -1.0, None, ALU.mult)
                elif bit < 16:
                    op(V.tensor_scalar, k_, k_, pbit[:, bit - 9:bit - 8], None, ALU.mult)

            def far_stage(j):
                a, b = at[0], 1 - at[0]
                far = 1 << (j - 9)
                for base in range(0, P, 2 * far):
                    for low in range(base, base + far, 32):
                        high = low + far
                        L, H = slice(low, low + 32), slice(high, high + 32)
                        op(V.tensor_copy, kh[L, :], key[a][H, :])
                        V.tensor_copy(th[L, :], tag[a][H, :]).then_inc(dve_step, n.up())
                        op(V.tensor_tensor, mk[L, :], key[a][L, :], kh[L, :], ALU.is_gt)
                        V.tensor_tensor(df[L, :], th[L, :], tag[a][L, :], ALU.subtract).then_inc(dve_step, n.up())
                        V.tensor_tensor(key[b][L, :], key[a][L, :], kh[L, :], ALU.min).then_inc(dve_step, n.up())
                        V.tensor_tensor(key[b][H, :], key[a][L, :], kh[L, :], ALU.max).then_inc(dve_step, n.up())
                        op(V.tensor_tensor, df[L, :], df[L, :], mk[L, :], ALU.mult)
                        op(V.tensor_tensor, tag[b][L, :], tag[a][L, :], df[L, :], ALU.add)
                        V.tensor_tensor(tag[b][H, :], th[L, :], df[L, :], ALU.subtract).then_inc(dve_step, n.up())
                settle()
                at[0] = b

            spare = center[:, :, :].rearrange("p s a -> p (s a)")
            kh, th = spare[:, 0:SC], spare[:, SC:2 * SC]
            mk, df = spare[:, 2 * SC:3 * SC], half

            for phase in range(1, 17):
                if phase == 15:
                    a, b = at[0], 1 - at[0]
                    op(V.tensor_scalar, key[a], key[a], pbit[:, 5:6], None, ALU.mult)
                    op(V.tensor_scalar, h_i, key[a].bitcast(I32), (1 << LOWBITS) - 1, None, ALU.bitwise_and)
                    op(V.tensor_scalar, tag[b], h_i, tmp[:, 0:1], None, ALU.add)
                    op(V.tensor_scalar, h_i, key[a].bitcast(I32), LOWBITS, None, ALU.logical_shift_right)
                    op(V.tensor_scalar, key[b], h_i, float(-BIAS), None, ALU.add)
                    tagged[0] = True
                    at[0] = b
                    flip(15)
                else:
                    if phase > 1:
                        flip(phase - 1)
                    flip(phase)
                for j in range(phase - 1, 13, -1):
                    far_stage(j)
                if phase > 9:
                    turn_blocks()
                    for j in range(min(phase - 1, 13), 8, -1):
                        column_stage(j - 9)
                    turn_blocks()
                for j in range(min(phase - 1, 8), -1, -1):
                    column_stage(j)
            if at[0]:
                op(V.tensor_copy, key[0], key[1])
                op(V.tensor_copy, tag[0], tag[1])
            settle()
            dve.sem_inc(sort_done, 1)

            first, ends, rep = score_max, gate_sum, weight_sum

            def make_order(d, end, same, pick, final, cont, side_final, jk):
                e, f, r = same, pick, for_counts
                op(V.tensor_scalar, f[:, :], d, d[:, 0:1], None, ALU.is_equal)
                op(V.tensor_tensor, cont[:, 1:2], d[:, 0:1], end[:, 0:1], ALU.is_equal)
                op(V.tensor_tensor, notn[:, :], d[:, EC - 1:EC], end[:, 1:2], ALU.not_equal)
                op(V.tensor_tensor, cont[:, 0:1], f[:, EC - 1:EC], cont[:, 1:2], ALU.mult)
                op(V.tensor_scalar, tmp[:, 2:3], notn[:, :], -1.0, 1.0, ALU.mult, ALU.add)
                op(V.tensor_tensor, tmp[:, 2:3], tmp[:, 2:3], f[:, EC - 1:EC], ALU.mult)
                op(V.tensor_scalar, tmp[:, 2:3], tmp[:, 2:3], -1.0, 1.0, ALU.mult, ALU.add)
                op(V.tensor_scalar, tmp[:, 3:4], pidx[:, :], float(N + 2 * K * P), None, ALU.add)
                op(V.tensor_tensor, tmp[:, 1:2], d[:, 0:1], tmp[:, 3:4], ALU.subtract)
                op(V.tensor_tensor, tmp[:, 1:2], tmp[:, 1:2], tmp[:, 2:3], ALU.mult)
                op(V.tensor_tensor, side_final[:, :], tmp[:, 1:2], tmp[:, 3:4], ALU.add)
                op(V.tensor_tensor, e[:, 0:EC - 1], d[:, 0:EC - 1], d[:, 1:EC], ALU.not_equal)
                op(V.memset, e[:, EC - 1:EC], 1.0)
                op(V.tensor_tensor, pick[:, :], f[:, :], e[:, :], ALU.mult)
                op(V.tensor_tensor, r, e[:, :], pick[:, :], ALU.subtract)
                op(V.tensor_tensor, r[:, EC - 1:EC], r[:, EC - 1:EC], notn[:, :], ALU.mult)
                op(V.memset, same[:, 0:1], 0.0)
                op(V.tensor_tensor, same[:, 1:EC], d[:, 1:EC], d[:, 0:EC - 1], ALU.is_equal)
                op(V.tensor_tensor, d, d, jk, ALU.subtract)
                op(V.tensor_tensor, d, d, r, ALU.mult)
                op(V.tensor_tensor, final[:, :], d, jk, ALU.add)

            d = weight_sum[:, 1:1 + EC]
            op(V.tensor_copy, d, dst_i[:, :])
            op(V.tensor_copy, endf[:, :], ends_d[:, :])
            make_order(d, endf, same_d, pick_d, final_d, cont_d, side_final_d, junk)
            dve.wait_ge(sort_loaded, 16 * 10)
            for c in range(EQ + 1, EC):
                for array in (score_max, gate_sum):
                    op(V.tensor_copy, array[:, 1 + c:2 + c], array[:, c:1 + c])
            op(V.tensor_copy, slot_s[:, :], gate_sum[:, 1:1 + EC])
            make_order(score_max[:, 1:1 + EC], ends_s, same_s, pick_s, final_s, cont_s, side_final_s, junk)
            settle()
            dve.sem_inc(ready_s, 1)
            op(V.memset, mask_rep[:, :, :, :], 0.0)
            op(V.memset, msg[:, :, :, :], 0.0)
            settle()
            dve.sem_inc(sort_done, 1)
            dve.wait_ge(side_turned, 1)
            V.tensor_copy(waT[:, :], side_ps[0:D, 0:D]).then_inc(side_ready, 1)
            dve.wait_ge(side_turned, 2)
            op(V.tensor_copy, src_w[:, 0:1], side_ps[0:D, 0:1])
            op(V.tensor_copy, dst_w[:, 0:1], side_ps[0:D, 1:2])

            def turn_masks(cont, turned_at):
                op(V.tensor_copy, tails[:, 0, :], cont[:, 0:1].to_broadcast([P, W]))
                op(V.tensor_copy, tails[:, 1, :], cont[:, 1:2].to_broadcast([P, W]))
                settle()
                dve.sem_inc(side_ready, 1)
                dve.wait_ge(side_turned, turned_at)
                op(V.tensor_copy, maskT[:, 0, :], side_ps[0:W, 0:P])
                op(V.tensor_copy, maskT[:, 1, :], side_ps[0:W, P:2 * P])

            def carry_sums(turned_at, tail, counts=None):
                op(V.memset, tails[:, 0, D:W], 0.0)
                op(V.memset, chainT[:, :, 0:1], 0.0)
                op(V.tensor_copy, tails[:, 0, 0:D], tail)
                if counts is not None:
                    op(V.memset, tails[:, 1, :], 0.0)
                    op(V.tensor_copy, tails[:, 1, 0:1], counts)
                settle()
                dve.sem_inc(side_ready, 1)
                dve.wait_ge(side_turned, turned_at)
                for c in range(1 if counts is None else 2):
                    op(V.tensor_tensor_scan, chainT[:, c, 1:P + 1], maskT[:, 0, :],
                       side_ps[0:W, c * P:(c + 1) * P], 0.0, ALU.mult, ALU.add)
                    op(V.tensor_tensor, inT[:, c, :], chainT[:, c, 0:P], maskT[:, 1, :], ALU.mult)
                settle()
                dve.sem_inc(side_ready, 1)
                dve.wait_ge(side_turned, turned_at + 1)

            def degrees(same, pick):
                deg = weight_sum[:, 1:1 + EC]
                op(V.tensor_tensor_scan, deg, same[:, :], real[:, :], 0.0, ALU.mult, ALU.add)
                op(V.tensor_copy, side_s[:, 16:17], weight_sum[:, EC:EC + 1])
                op(V.tensor_tensor, for_counts, deg, pick[:, :], ALU.mult)
                op(V.tensor_reduce, side_s[:, 17:18], for_counts, AX, ALU.add)
                op(V.tensor_scalar, deg, deg, 1.0, None, ALU.max)
                op(V.reciprocal, rdeg[:, :], deg)

            def beside(f, *a, **k):
                return f(*a, **k).then_inc(dve_step, n.up())

            def row_stats(xt, s):
                for t in range(K):
                    beside(V.bn_stats, stats[:, s, t, :], xt[:, t, :])

            def moments(s):
                mean_a, sq_a, mean_b, sq_b = (stats[:, s, :, k] for k in (1, 2, 4, 5))
                op(V.tensor_tensor, rowsum[:, s, :], mean_a, mean_b, ALU.add)
                beside(V.tensor_tensor, apart[:, s, :], mean_a, mean_b, ALU.subtract)
                beside(V.tensor_tensor, sumsq[:, s, :], sq_a, sq_b, ALU.add)
                op(V.tensor_scalar, negmean[:, s, :], rowsum[:, s, :], -0.5, None, ALU.mult)
                beside(V.scalar_tensor_tensor, out=apart[:, s, :], in0=apart[:, s, :], scalar=D / 4.0,
                       in1=apart[:, s, :], op0=ALU.mult, op1=ALU.mult)
                settle()
                V.tensor_tensor(sumsq[:, s, :], sumsq[:, s, :], apart[:, s, :], ALU.add).then_inc(summed, 1)

            def center_rows(xt, s):
                op(V.tensor_tensor, tk(center[:, s, :]), xt, bc_f(negmean[:, s, :]), ALU.add)

            def scale_of(m, s):
                dve.wait_ge(deviated, m)
                op(V.reciprocal, rstd[:, s, :], std[:, s, :])

            def pick_side(pick, i, s, source, into):
                op(V.tensor_tensor, picked[:, :, :], source, bc_t(pick[:, cols(i, s)]), ALU.mult)
                op(V.tensor_reduce, side_part[:, :], picked[:, :, :], AX, ALU.add)
                op(V.tensor_tensor, into, into, side_part[:, :], ALU.add)

            def edge_back(layer, i, s, slot, norm, same_at, weights, pick):
                scale_of(norm, slot)
                op(V.tensor_tensor, coef[:, s, :], rstd[:, slot, :], weights[:, cols(i, s)], ALU.mult)
                to = by_slot(msg[:, s, :, 1:K + 1])
                h = tk(hrow[:, s, :]) if layer == 1 else to
                op(V.scalar_tensor_tensor, out=h, in0=tk(center[:, slot, :]), scalar=0.0,
                   in1=bc_f(coef[:, s, :]), op0=ALU.max, op1=ALU.mult)
                if layer == 1:
                    op(V.tensor_tensor, to, h, tk(kept[:, fcols(i, s)]), ALU.mult)
                op(V.tensor_copy, msg[:, s, :, 0:1], run[:, 1 - s, :, K:K + 1])
                dve.wait_ge(mask_made, i * 2 + (same_at + s + 1))
                dve.wait_ge(sums_kept, i * 2 + (min(layer, 2) * CHUNKS + s + 1))
                settle()
                V.tensor_tensor_scan(flat(run[:, s, :, :]), flat(mask_rep[:, s, :, :]), flat(msg[:, s, :, :]),
                                     0.0, ALU.mult, ALU.add).then_inc(scanned, 1)
                dve.wait_ge(scanned, i * 2 + (same_at + s + 3))
                if pick is not None:
                    pick_side(pick, i, s, run[:, s, :, 1:K + 1], side_sum[:, :])

            for layer, pick, weights, cont, side_final in ((0, pick_d, wt, cont_d, side_final_d),
                                                           (1, pick_s, real, cont_s, side_final_s)):
                turn_masks(cont, 3 + 3 * layer)

                def front(i, s):
                    if layer == 0:
                        dve.wait_ge(got_free, i * 2 + (s + 3))
                        rows = tk(kept[:, fcols(i, s)])
                        row_stats(rows, s)
                        moments(s)
                        center_rows(rows, s)
                    else:
                        dve.wait_ge(landed[s], i * (16 * K) + (2 * LANDS + 16 * K))
                        rows = tk(got[:, s, 0:K * D])
                        row_stats(rows, s)
                        moments(s)
                        center_rows(rows, s)
                        settle()
                        dve.sem_inc(got_free, 1)

                def back(i, s):
                    edge_back(layer, i, s, s, i * 2 + (NORMS[layer] + s + 1), layer * CHUNKS, weights, pick)

                if layer == 1:
                    dve.wait_ge(got_free, 2 + 2 * CHUNKS)
                front(0, 0)
                with dve.Fori(0, PAIRS - 1) as i:
                    n.enter(i, 0, 54 if layer == 0 else 56)
                    front(i, 1)
                    back(i, 0)
                    front(i + 1, 0)
                    back(i, 1)
                    n.leave(PAIRS - 1)
                front(PAIRS - 1, 1)
                back(PAIRS - 1, 0)
                back(PAIRS - 1, 1)
                carry_sums(4 + 3 * layer, run[:, 1, :, K])
                if layer:
                    dve.wait_ge(side_scattered, 16 * layer)
                settle()
                V.tensor_tensor(side_out[:, :], side_sum[:, :], side_ps[:, 0:D], ALU.add).then_inc(side_made, 1)
                dve.wait_ge(side_made, layer + 1)
                op(V.memset, side_sum[:, :], 0.0)
                dve.wait_ge(sums_kept, (layer + 1) * CHUNKS + 2)
                op(V.memset, run[:, :, :, :], 0.0)

            turn_masks(cont_d, 9)
            op(V.tensor_scalar, d, same_d[:, :], BIG, -BIG, ALU.mult, ALU.add)
            op(V.tensor_scalar, cap[:, :], same_d[:, :], BIG, None, ALU.mult)
            op(V.tensor_tensor, cap[:, :], cap[:, :], d, ALU.add)
            degrees(same_d, pick_d)
            op(V.memset, score_max[:, 0:1], 0.0)
            op(V.memset, mask_rep[:, 0, :, :], 0.0)
            op(V.memset, mask_rep[:, 1, :, :], -BIG)
            settle()
            dve.sem_inc(masks_set, 1)

            def fronts(g, s):
                rows = tk(got[:, s, 0:K * D]), tk(got_dst[:, s, :])
                dve.wait_ge(landed[s], lands(g, s, 3 * LANDS))
                row_stats(rows[0], 0)
                dve.wait_ge(landed_dst[s], lands(g, s, 0))
                row_stats(rows[1], 1)
                moments(slice(0, 2))
                center_rows(rows[0], 0)
                center_rows(rows[1], 1)
                settle()
                dve.sem_inc(got_free, 1)
                dve.sem_inc(got_dst_free, 1)

            def lands(g, s, before):
                return (g - s) * (8 * K) + (16 * K + before)

            def backs(g, wait_turned=True):
                scale_of(g + (NORMS[2] + 1), slice(0, 2))
                for s in range(2):
                    if wait_turned:
                        dve.wait_ge(turned, g * 8 - 4 + 4 * s)
                    settle()
                    V.scalar_tensor_tensor(out=tk(hrow[:, s, :]), in0=tk(center[:, s, :]), scalar=0.0,
                                           in1=bc_f(rstd[:, s, :]), op0=ALU.max,
                                           op1=ALU.mult).then_inc(hrow_made, 1)

            def scores(i, s, last=False):
                dve.wait_ge(shares_made, i * 2 + (s + 1))
                c = cols(i, s)
                before = bass.ds(i * (2 * K) + s * K, 1)
                prev = bass.ds(i * (2 * K) + s * K, K)
                now = bass.ds(i * (2 * K) + s * K + 1, K)
                sh = share_ps[:, 0:2 * K].rearrange("p (t c) -> p t c", c=2)
                shd = share_ps[:, 2 * K:4 * K].rearrange("p (t c) -> p t c", c=2)
                op(V.tensor_tensor, score[:, :], sh[:, :, 0], w1t[:, c], ALU.mult)
                op(V.tensor_tensor, share[:, :], sh[:, :, 1], w1t[:, c], ALU.mult)
                op(V.tensor_tensor, score[:, :], score[:, :], shd[:, :, 0], ALU.add)
                op(V.tensor_copy, gate_dst[:, s, :], shd[:, :, 1])
                settle()
                dve.sem_inc(shares_used, 1)
                op(V.scalar_tensor_tensor, out=score[:, :], in0=score[:, :], scalar=0.01,
                   in1=score[:, :], op0=ALU.mult, op1=ALU.max)
                if last:
                    op(V.tensor_tensor, share[:, :], share[:, :], real[:, c], ALU.mult)
                    op(V.tensor_tensor, score[:, :], score[:, :], real[:, c], ALU.mult)
                    op(V.tensor_scalar, rowsum[:, 0, :], real[:, c], -LOW, LOW, ALU.mult, ALU.add)
                    op(V.tensor_tensor, score[:, :], score[:, :], rowsum[:, 0, :], ALU.add)
                op(V.tensor_tensor_scan, gate_sum[:, now], same_d[:, c], share[:, :],
                   gate_sum[:, before], ALU.mult, ALU.add)
                op(V.tensor_tensor_scan, score_max[:, now], cap[:, c], score[:, :],
                   score_max[:, before], ALU.min, ALU.max)
                op(V.tensor_tensor, expo[:, 0, :], score_max[:, prev], score_max[:, now], ALU.subtract)
                op(V.tensor_scalar, expo[:, 0, :], expo[:, 0, :], 0.0, None, ALU.min)
                settle()
                V.tensor_tensor(expo[:, 1, :], score[:, :], score_max[:, now],
                                ALU.subtract).then_inc(expo_made, 1)
                dve.wait_ge(exp_done, i * 2 + (s + 1))
                V.tensor_tensor(decay[:, s, :], wexp[:, s, 0, :], same_d[:, c], ALU.mult).then_inc(decay_made, 1)

            run_max = run[:, 1, :, :]
            run_sum = run[:, 0, :, :]

            def sums(i, s):
                c = cols(i, s)
                before = bass.ds(i * (2 * K) + s * K, 1)
                now = bass.ds(i * (2 * K) + s * K + 1, K)
                g1 = i * 2 + (s + 1)
                dve.wait_ge(decay_made, g1)
                op(V.tensor_tensor_scan, weight_sum[:, now], decay[:, s, :], wexp[:, s, 1, :],
                   weight_sum[:, before], ALU.mult, ALU.add)
                dve.wait_ge(proj_made, g1)
                op(V.tensor_tensor, by_slot(msg[:, 0, :, 1:K + 1]), tk(value_ps[:, 0:K * D]),
                   bc_f(wexp[:, s, 1, :]), ALU.mult)
                op(V.tensor_copy, msg[:, 0, :, 0:1], run_sum[:, :, K:K + 1])
                settle()
                dve.sem_inc(value_free, 1)
                dve.wait_ge(decay_rep, g1)
                V.tensor_tensor_scan(flat(run_sum), flat(mask_rep[:, 0, :, :]), flat(msg[:, 0, :, :]),
                                     0.0, ALU.mult, ALU.add).then_inc(scanned, 1)
                dve.wait_ge(feat_free, g1 + 1)
                op(V.tensor_copy, msg[:, 1, :, 0:1], run_max[:, :, K:K + 1])
                settle()
                V.tensor_tensor_scan(flat(run_max), flat(mask_rep[:, 1, :, :]), flat(msg[:, 1, :, :]),
                                     0.0, ALU.min, ALU.max).then_inc(gate_scanned, 1)
                dve.wait_ge(gate_scanned, g1 + 1)
                op(V.tensor_tensor, by_slot(picked[:, :, :]), by_slot(run_max[:, :, 1:K + 1]),
                   gmax_w[:, :].unsqueeze(1).to_broadcast([P, K, D]), ALU.mult)
                op(V.tensor_reduce, gate[:, :], by_slot(picked[:, :, :]), AX, ALU.add)
                op(V.tensor_tensor, coef[:, s, :], gate_sum[:, now], rdeg[:, c], ALU.mult)
                op(V.tensor_tensor, coef[:, s, :], coef[:, s, :], gate_dst[:, s, :], ALU.add)
                settle()
                V.tensor_tensor(gate[:, :], gate[:, :], coef[:, s, :], ALU.add).then_inc(gate_made, 1)
                dve.wait_ge(scanned, g1 + (2 * CHUNKS + 2))
                pick_side(pick_d, i, s, run_sum[:, :, 1:K + 1], side_sum[:, :])
                pick_side(pick_d, i, s, run_max[:, :, 1:K + 1], side_max[:, :])
                dve.wait_ge(gate_exp, g1)
                op(V.tensor_scalar, coef[:, s, :], weight_sum[:, now], 1e-30, None, ALU.max)
                op(V.scalar_tensor_tensor, out=coef[:, s, :], in0=gexp[:, :], scalar=1.0,
                   in1=coef[:, s, :], op0=ALU.add, op1=ALU.mult)
                op(V.reciprocal, rowsum[:, 0, :], coef[:, s, :])
                settle()
                V.tensor_tensor(tk(kept[:, fcols(i, s)]), by_slot(run_sum[:, :, 1:K + 1]),
                                bc_f(rowsum[:, 0, :]), ALU.mult).then_inc(kept_made, 1)
                dve.wait_ge(kept_made, g1)

            def attend(i, s, more=True, more2=True):
                g = i * 2 + s
                ni, ns = (i, 1) if s == 0 else (i + 1, 0)
                if more:
                    backs(g + 1)
                if more2:
                    fronts(g + 2, s)
                sums(i, s)
                if more:
                    scores(ni, ns, last=not more2)

            fronts(0, 0)
            backs(0, wait_turned=False)
            op(V.tensor_copy, tmp[:, 0:1], tmp[:, 0:1])
            fronts(1, 1)
            scores(0, 0)
            op(V.tensor_copy, side_s[:, 6:7], gate_dst[:, 0, 0:1])
            with dve.Fori(0, PAIRS - 1) as i:
                n.enter(i, 0, 124)
                for s in range(2):
                    attend(i, s)
                n.leave(PAIRS - 1)
            attend(PAIRS - 1, 0, more2=False)
            attend(PAIRS - 1, 1, more=False, more2=False)

            op(V.tensor_copy, tails[:, 0, 0:D], run_sum[:, :, K])
            op(V.tensor_copy, tails[:, 0, D:W], weight_sum[:, EC:EC + 1])
            op(V.memset, tails[:, 1, :], 0.0)
            op(V.tensor_copy, tails[:, 1, 0:D], run_max[:, :, K])
            op(V.memset, tails[:, 2, :], 0.0)
            op(V.tensor_copy, tails[:, 2, 0:1], gate_sum[:, EC:EC + 1])
            op(V.tensor_copy, tails[:, 2, 1:2], side_s[:, 16:17])
            op(V.tensor_copy, tails[:, 3, :], score_max[:, EC:EC + 1].to_broadcast([P, W]))
            settle()
            dve.sem_inc(side_ready, 1)
            op(V.tensor_scalar, capT[:, :], maskT[:, 0, :], BIG, None, ALU.mult)
            op(V.tensor_scalar, maskT[:, 2, :], maskT[:, 0, :], BIG, -BIG, ALU.mult, ALU.add)
            op(V.tensor_tensor, capT[:, :], capT[:, :], maskT[:, 2, :], ALU.add)
            op(V.tensor_scalar, maskT[:, 2, :], maskT[:, 1, :], BIG, None, ALU.mult)
            op(V.tensor_scalar, expT[:, 0, :], maskT[:, 1, :], BIG, -BIG, ALU.mult, ALU.add)
            op(V.tensor_tensor, maskT[:, 2, :], maskT[:, 2, :], expT[:, 0, :], ALU.add)
            op(V.memset, chainT[:, :, 0:1], 0.0)
            for k, array in enumerate((score_max, gate_sum, weight_sum)):
                op(V.tensor_tensor, for_counts, array[:, 1:1 + EC], pick_d[:, :], ALU.mult)
                op(V.tensor_reduce, side_s[:, 18 + k:19 + k], for_counts, AX, ALU.add)
            dve.wait_ge(side_turned, 10)

            def ps(c):
                return side_ps[0:W, c * P:(c + 1) * P]

            op(V.tensor_tensor_scan, chainT[:, 3, 1:P + 1], capT[:, :], ps(3), 0.0, ALU.min, ALU.max)
            op(V.tensor_tensor, expT[:, 0, :], chainT[:, 3, 0:P], chainT[:, 3, 1:P + 1], ALU.subtract)
            op(V.tensor_scalar, expT[:, 0, :], expT[:, 0, :], 0.0, None, ALU.min)
            settle()
            V.tensor_tensor(expT[:, 1, :], ps(3), chainT[:, 3, 1:P + 1], ALU.subtract).then_inc(side_act, 1)
            dve.wait_ge(side_acted, 1)
            op(V.tensor_tensor, wexpT[:, 0, :], wexpT[:, 0, :], maskT[:, 0, :], ALU.mult)
            op(V.tensor_tensor, wexpT[:, 1, :], wexpT[:, 1, :], ps(0), ALU.mult)
            op(V.tensor_tensor_scan, chainT[:, 0, 1:P + 1], wexpT[:, 0, :], wexpT[:, 1, :], 0.0, ALU.mult, ALU.add)
            op(V.tensor_tensor_scan, chainT[:, 1, 1:P + 1], capT[:, :], ps(1), 0.0, ALU.min, ALU.max)
            op(V.tensor_tensor_scan, chainT[:, 2, 1:P + 1], maskT[:, 0, :], ps(2), 0.0, ALU.mult, ALU.add)
            op(V.tensor_tensor, inT[:, 0, :], chainT[:, 0, 0:P], maskT[:, 1, :], ALU.mult)
            op(V.tensor_tensor, inT[:, 1, :], chainT[:, 1, 0:P], maskT[:, 2, :], ALU.min)
            op(V.tensor_tensor, inT[:, 2, :], chainT[:, 2, 0:P], maskT[:, 1, :], ALU.mult)
            op(V.tensor_tensor, inT[:, 3, :], chainT[:, 3, 0:P], maskT[:, 2, :], ALU.min)
            op(V.tensor_scalar, inT[:, 3, :], inT[:, 3, :], LOW, None, ALU.max)
            settle()
            dve.sem_inc(side_ready, 1)
            dve.wait_ge(side_turned, 11)

            def back_ps(c, a, b):
                return side_ps[:, c * P + a:c * P + b]

            op(V.tensor_tensor, side_s[:, 7:8], side_s[:, 18:19], back_ps(3, 0, 1), ALU.max)
            op(V.tensor_tensor, side_s[:, 8:9], side_s[:, 18:19], side_s[:, 7:8], ALU.subtract)
            settle()
            V.tensor_tensor(side_s[:, 9:10], back_ps(3, 0, 1), side_s[:, 7:8], ALU.subtract).then_inc(side_act, 1)
            dve.wait_ge(side_acted, 2)
            op(V.tensor_scalar, side_part[:, :], back_ps(0, 0, D), side_s[:, 11:12], None, ALU.mult)
            op(V.scalar_tensor_tensor, out=side_sum[:, :], in0=side_sum[:, :], scalar=side_s[:, 10:11],
               in1=side_part[:, :], op0=ALU.mult, op1=ALU.add)
            op(V.tensor_scalar, side_s[:, 12:13], back_ps(0, D, W), side_s[:, 11:12], None, ALU.mult)
            op(V.scalar_tensor_tensor, out=side_s[:, 12:13], in0=side_s[:, 20:21], scalar=side_s[:, 10:11],
               in1=side_s[:, 12:13], op0=ALU.mult, op1=ALU.add)
            op(V.tensor_scalar, side_s[:, 12:13], side_s[:, 12:13], 1e-30, None, ALU.max)
            op(V.tensor_tensor, side_max[:, :], side_max[:, :], back_ps(1, 0, D), ALU.max)
            op(V.tensor_tensor, side_part[:, :], side_max[:, :], gmax_w[:, :], ALU.mult)
            op(V.tensor_reduce, side_s[:, 13:14], side_part[:, :], AX, ALU.add)
            op(V.tensor_tensor, side_s[:, 21:22], side_s[:, 19:20], back_ps(2, 0, 1), ALU.add)
            op(V.tensor_tensor, side_s[:, 22:23], side_s[:, 17:18], back_ps(2, 1, 2), ALU.add)
            op(V.tensor_scalar, side_s[:, 22:23], side_s[:, 22:23], 1.0, None, ALU.max)
            op(V.reciprocal, side_s[:, 23:24], side_s[:, 22:23])
            op(V.scalar_tensor_tensor, out=side_s[:, 21:22], in0=side_s[:, 21:22], scalar=side_s[:, 23:24],
               in1=side_s[:, 13:14], op0=ALU.mult, op1=ALU.add)
            settle()
            V.tensor_tensor(side_s[:, 14:15], side_s[:, 21:22], side_s[:, 6:7], ALU.add).then_inc(side_act, 1)
            dve.wait_ge(side_acted, 3)
            op(V.scalar_tensor_tensor, out=side_s[:, 12:13], in0=side_s[:, 15:16], scalar=1.0,
               in1=side_s[:, 12:13], op0=ALU.add, op1=ALU.mult)
            op(V.reciprocal, side_s[:, 13:14], side_s[:, 12:13])
            dve.wait_ge(side_scattered, 32)
            settle()
            V.tensor_scalar(side_out[:, :], side_sum[:, :], side_s[:, 13:14], None, ALU.mult).then_inc(side_made, 1)

            dve.wait_ge(side_made, 3)

            op(V.memset, side_sum[:, :], 0.0)
            op(V.memset, run[:, :, :, :], 0.0)
            op(V.memset, mask_rep[:, :, :, :], 0.0)
            turn_masks(cont_s, 12)
            degrees(same_s, pick_s)
            settle()
            dve.sem_inc(masks_set, 1)

            def norm_no(i, m):
                return i * 6 + (NORMS[3] + m + 1)

            def mixed_front(i, m):
                s = m // 3
                if m % 3 == 0:
                    rows = tk(got[:, s, 0:K * D])
                    dve.wait_ge(landed[s], i * (16 * K) + (4 * LANDS + 16 * K))
                    row_stats(rows, m % 2)
                    moments(m % 2)
                    center_rows(rows, m % 2)
                    settle()
                    dve.sem_inc(got_free, 1)
                else:
                    j = 2 * s + m % 3 - 1
                    dve.wait_ge(x_loaded[j], i * 32 + 32)
                    row_stats(tk(rowin[:, j * K * D:(j + 1) * K * D]), m % 2)
                    moments(m % 2)

            def mixed_back(i, m):
                s, c = m // 3, m % 2
                if m % 3 == 0:
                    edge_back(3, i, s, c, norm_no(i, m), 3 * CHUNKS, real, None)
                    return
                scale_of(norm_no(i, m), c)
                settle()
                V.tensor_tensor(shift[:, c, :], negmean[:, c, :], rstd[:, c, :], ALU.mult).then_inc(shifted, 1)

            def add_rows(i, j, start=False):
                if not (start and j < 2):
                    dve.wait_ge(outs_stored[j % 2], i * 64 + 32 * (j // 2))
                dve.wait_ge(rows_made, i * 4 + (j + 1))
                V.tensor_tensor(outrow[:, j % 2, :], rowin[:, j * K * D:(j + 1) * K * D], hrow[:, j % 2, :],
                                ALU.add).then_inc(out_made, 1)
                dve.wait_ge(out_made, i * 4 + (j + 1))
                dve.sem_inc(x_used, 1)

            def mixed(i, start=False, last=False):
                for m in range(6):
                    if m < 5:
                        mixed_front(i, m + 1)
                    elif not last:
                        mixed_front(i + 1, 0)
                    mixed_back(i, m)
                    if m == 0 and not start:
                        add_rows(i - 1, 3)
                    elif m - 1 in STAGE_OF:
                        add_rows(i, STAGE_OF.index(m - 1), start)

            mixed_front(0, 0)
            mixed(0, start=True)
            with dve.Fori(1, PAIRS - 1) as i:
                n.enter(i, 1, 128)
                mixed(i)
                n.leave(PAIRS - 2)
            mixed(PAIRS - 1, last=True)
            add_rows(PAIRS - 1, 3)
            for s in range(2):
                dve.wait_ge(outs_stored[s], 16 * TILES)

            def means(i, s):
                c = tk(kept[:, fcols(i, s)])
                dve.wait_ge(sums_kept, i * 2 + (2 * CHUNKS + s + 3))
                dve.wait_ge(outrow_free, i * 2 + (3 * CHUNKS + s + 1))
                V.tensor_tensor(tk(outrow[:, s, :]), c, bc_f(rdeg[:, cols(i, s)]), ALU.mult).then_inc(outrow_made, 1)
                pick_side(pick_s, i, s, by_feature(c), side_sum[:, :])

            with dve.Fori(0, PAIRS) as i:
                n.enter(i, 0, 6)
                for s in range(2):
                    means(i, s)
                n.leave(PAIRS)
            carry_sums(13, run[:, 1, :, K], side_s[:, 16:17])
            op(V.tensor_tensor, side_s[:, 0:1], side_s[:, 17:18], side_ps[:, P:P + 1], ALU.add)
            op(V.tensor_scalar, side_s[:, 0:1], side_s[:, 0:1], 1.0, None, ALU.max)
            op(V.reciprocal, side_s[:, 1:2], side_s[:, 0:1])
            op(V.tensor_tensor, side_sum[:, :], side_sum[:, :], side_ps[:, 0:D], ALU.add)
            dve.wait_ge(side_scattered, 48)
            settle()
            V.tensor_scalar(side_out[:, :], side_sum[:, :], side_s[:, 1:2], None, ALU.mult).then_inc(side_made, 1)


def kernel(x, src, dst, edge_attr_64, edge_weight, edge_weight1, L2_gnn_Wa, L2_gnn_att_w, L2_gnn_Wg,
           L2_gnn_gate_w):
    import numpy as np
    import concourse.bacc as bacc
    from concourse.bass_utils import run_bass_kernel_spmd

    arrays = {
        "x_in": x, "src_in": np.reshape(src, (-1, 1)), "dst_in": np.reshape(dst, (-1, 1)),
        "attr_in": edge_attr_64, "w_in": np.reshape(edge_weight, (-1, 1)), "w1_in": edge_weight1,
        "Wa_in": L2_gnn_Wa, "att_in": L2_gnn_att_w, "Wg_in": L2_gnn_Wg, "gate_in": L2_gnn_gate_w,
    }
    arrays = {name: np.ascontiguousarray(a) for name, a in arrays.items()}
    N = arrays["x_in"].shape[0]
    nc = bacc.Bacc("TRN2", target_bir_lowering=False, num_devices=1)
    ins = [nc.dram_tensor(name, a.shape, mybir.dt.from_np(a.dtype), kind="ExternalInput").ap()
           for name, a in arrays.items()]
    out = nc.dram_tensor("x_out", (N + (2 * K + 1) * P, D), F32, kind="ExternalOutput").ap()
    gnn_kernel(nc, *ins, out)
    result = run_bass_kernel_spmd(nc, [arrays], core_ids=[0])
    return result.results[0]["x_out"][:N]
```

```python
from contextlib import ExitStack

import concourse.bass as bass
from concourse import mybir

P = 128
D = 64
W = D + 1
K = 14
EPS = 1e-5
BIG = 3.0e38
LOW = -1.0e30
GROUPS = [(0, 4), (4, 4), (8, 4), (12, 2)]
SC = 512
LOWBITS = 14
BIAS = 512
FILL = 130000

F32 = mybir.dt.float32
I32 = mybir.dt.int32
ALU = mybir.AluOpType
ACT = mybir.ActivationFunctionType
AX = mybir.AxisListType.X


class Count:

    def __init__(self):
        self.base, self.n = 0, 0

    def up(self):
        self.n += 1
        return 1

    def now(self):
        return self.base + self.n

    def enter(self, i, first, per):
        self.start, self.per = self.base + self.n, per
        self.base, self.n = (i - first) * per + self.start, 0

    def leave(self, times):
        assert self.n == self.per, f"the body counts {self.n}, not {self.per}"
        self.base, self.n = self.start + self.per * times, 0


def gnn_kernel(nc, x, src, dst, attr, w, w1, Wa, att_w, Wg, gate_w, out):
    N, E = x.shape[0], src.shape[0]
    EQ, ER = divmod(E, P)
    NQ, NR = divmod(N, P)
    PAIRS = -(-(EQ + 1) // (2 * K))
    CHUNKS = 2 * PAIRS
    EC = K * CHUNKS
    TILES = 2 * CHUNKS
    assert PAIRS >= 3 and EC - K < EQ and K * (TILES - 1) < NQ < NQ + 1 <= K * TILES
    assert 32 * EC <= 2 ** LOWBITS and EC <= SC and N < FILL and (FILL + BIAS) << LOWBITS < 0x7F800000
    JUNK = (2 * K + 1) * P
    assert out.shape[0] == N + JUNK

    def runs(view, q, r):
        a = view[0:r * (q + 1), :].rearrange("(p t) d -> p t d", t=q + 1)
        b = view[r * (q + 1):r * (q + 1) + (P - r) * q, :].rearrange("(p t) d -> p t d", t=q)
        return a, b

    with ExitStack() as ctx:
        def sb(name, shape, dt=F32):
            return ctx.enter_context(nc.sbuf_tensor("t_" + name, shape, dt))

        def psum(name, shape):
            return ctx.enter_context(nc.psum_tensor("p_" + name, shape, F32))

        def sem(name):
            return ctx.enter_context(nc.semaphore(name))

        nodes = nc.dram_tensor("nodes", (N + JUNK, D), F32).ap()
        filters = nc.dram_tensor("filters", (P * EC, W), F32).ap()
        sorted_src = nc.dram_tensor("sorted_src", (P * SC, 1), F32).ap()
        sorted_slot = nc.dram_tensor("sorted_slot", (P * SC, 1), F32).ap()

        dst_i = sb("dst_i", [P, EC], I32)
        src_i = sb("src_i", [P, EC], I32)
        wt = sb("w", [P, EC])
        w1t = sb("w1", [P, EC])
        same_d = sb("same_d", [P, EC])
        pick_d = sb("pick_d", [P, EC])
        final_d = sb("final_d", [P, EC], I32)
        slot_s = sb("slot_s", [P, EC], I32)
        cap = slot_s[:, :].bitcast(F32)
        dst_s = sb("dst_s", [P, EC], I32)
        same_s = sb("same_s", [P, EC])
        pick_s = sb("pick_s", [P, EC])
        final_s = sb("final_s", [P, EC], I32)
        real = sb("real", [P, EC])
        rdeg = sb("rdeg", [P, EC])
        score_max = sb("score_max", [P, 1 + EC])
        gate_sum = sb("gate_sum", [P, 1 + EC])
        weight_sum = sb("weight_sum", [P, 1 + EC])

        kept = sb("kept", [P, EC * D])
        stage = sb("stage", [P, 2, K], I32)
        stage_dst = sb("stage_dst", [P, 2, K], I32)
        stage_out = sb("stage_out", [P, 2, K], I32)
        got = sb("got", [P, 2, K * W])
        outrow = sb("outrow", [P, 2, K * D])
        got_dst = sb("got_dst", [P, 2, K * D])
        square = got_dst
        rowin = sb("rowin", [P, 4 * K * D])
        mask_rep = sb("mask_rep", [P, 2, D, K + 1])
        msg = sb("msg", [P, 2, D, K + 1])
        run = sb("run", [P, 2, D, K + 1])
        picked = sb("picked", [P, D, K])
        center = sb("center", [P, 2, K * D])
        hrow = sb("hrow", [P, 2, K * D])
        hT = rowin[0:D, :].rearrange("p (s a) -> p s a", s=2)
        filter_in = rowin[:, 0:2 * K * W].rearrange("p (s t w) -> p s t w", s=2, w=W)
        rowsum = sb("rowsum", [P, 4, K])
        negmean = sb("negmean", [P, 4, K])
        stats = sb("stats", [P, 2, K, 6])
        apart = sb("apart", [P, 2, K])
        sumsq = sb("sumsq", [P, 4, K])
        std = sb("std", [P, 4, K])
        rstd = sb("rstd", [P, 4, K])
        score = sb("score", [P, K])
        share = sb("share", [P, K])
        gate_dst = sb("gate_dst", [P, 2, K])
        expo = sb("expo", [P, 2, K])
        wexp = sb("wexp", [P, 2, 2, K])
        decay = sb("decay", [P, 2, K])
        gate = sb("gate", [P, K])
        gexp = sb("gexp", [P, K])
        coef = sb("coef", [P, 2, K])
        shift = sb("shift", [P, 2, K])

        words = msg[:, :, :, :].rearrange("p a f t -> p (a f t)")
        words2 = mask_rep[:, :, :, :].rearrange("p a f t -> p (a f t)")
        key = [words[:, 0:SC], words[:, SC:2 * SC]]
        tag = [words[:, 2 * SC:3 * SC], words2[:, 0:SC]]
        swap = words2[:, SC:SC + SC // 2]
        diff = words2[:, SC + SC // 2:2 * SC]
        word = words2[:, 2 * SC:3 * SC]

        pidx_i = sb("pidx_i", [P, 1], I32)
        pbit_i = sb("pbit_i", [P, 8], I32)
        pidx = sb("pidx", [P, 1])
        pbit = sb("pbit", [P, 8])
        ends_d = sb("ends_d", [P, 2], I32)
        ends_s = sb("ends_s", [P, 2])
        endf = sb("endf", [P, 2])
        cont_d, cont_s = sb("cont_d", [P, 2]), sb("cont_s", [P, 2])
        notn = sb("notn", [P, 1])
        side_final_d = sb("side_final_d", [P, 1], I32)
        side_final_s = sb("side_final_s", [P, 1], I32)
        tmp = sb("tmp", [P, 4])
        eps = sb("eps", [P, 1])
        ident = sb("ident", [P, P])
        wa_sb = sb("wa_sb", [D, D])
        WgWa = sb("WgWa", [D, 2 * D])
        att = sb("att", [D, 2])
        waT = sb("waT", [D, D])
        src_w = sb("src_w", [D, 2])
        dst_w = sb("dst_w", [D, 2])
        gmax_w = sb("gmax_w", [P, D])
        side_sum = sb("side_sum", [P, D])
        side_max = sb("side_max", [P, D])
        side_part = sb("side_part", [P, D])
        side_out = sb("side_out", [P, D])
        side_s = sb("side_s", [P, 24])
        room = hrow[:, :, :].rearrange("p s a -> p (s a)")

        def take(rows, at, n, width):
            return room[0:rows, at:at + n * width].rearrange("p (n w) -> p n w", n=n)

        tails = take(P, 0, 4, W)
        inT = take(W, 4 * W, 4, P)
        room2 = center[:, :, :].rearrange("p s a -> p (s a)")
        chainT = room2[0:W, 0:4 * (P + 1)].rearrange("p (n w) -> p n w", w=P + 1)
        expT = take(W, 4 * W + 4 * P, 2, P)
        wexpT = take(W, 4 * W + 6 * P, 2, P)
        assert 4 * W + 8 * P <= 2 * K * D
        maskT = sb("maskT", [W, 3, P])
        capT = room2[0:W, 4 * (P + 1):4 * (P + 1) + P]
        for_counts = picked[:, :, :].rearrange("p f t -> p (f t)")[:, 0:EC]
        assert D * K >= EC

        hT_ps = psum("hT_ps", [P, 2, 512])
        feat_ps = psum("feat_ps", [P, 1024])
        value_ps = psum("value_ps", [P, 1024])
        share_ps = psum("share_ps", [P, 512])
        side_ps = psum("side_ps", [P, 512])

        src_loaded, loaded, consts = sem("src_loaded"), sem("loaded"), sem("consts")
        src_ready = sem("src_ready")
        dve_step = sem("dve_step")
        masks_set = sem("masks_set")
        ready_d, ready_s = sem("ready_d"), sem("ready_s")
        sort_done, sort_stored, sort_loaded = sem("sort_done"), sem("sort_stored"), sem("sort_loaded")
        nodes_copied, zeroed = sem("nodes_copied"), sem("zeroed")
        filter_loaded = [sem(f"filter_loaded{s}") for s in range(2)]
        filter_stored = [sem(f"filter_stored{s}") for s in range(2)]
        filter_named = sem("filter_named")
        landed = [sem(f"landed{s}") for s in range(2)]
        landed_dst = [sem(f"landed_dst{s}") for s in range(2)]
        scattered = [sem(f"scattered{s}") for s in range(2)]
        side_scattered = sem("side_scattered")
        side_made = sem("side_made")
        staged = sem("staged")
        next_staged = sem("next_staged")
        out_staged = sem("out_staged")
        got_free = sem("got_free")
        got_dst_free = sem("got_dst_free")
        outrow_made, outrow_free = sem("outrow_made"), sem("outrow_free")
        centered, squared = sem("centered"), sem("squared")
        shifted, rows_made = sem("shifted"), sem("rows_made")
        summed, deviated = sem("summed"), sem("deviated")
        mask_made, scanned = sem("mask_made"), sem("scanned")
        sums_kept = sem("sums_kept")
        kept_made = sem("kept_made")
        hrow_made = sem("hrow_made")
        turned, turned_free = sem("turned"), sem("turned_free")
        shares_made, shares_used = sem("shares_made"), sem("shares_used")
        proj_made = sem("proj_made")
        feat_free, value_free = sem("feat_free"), sem("value_free")
        expo_made, exp_done = sem("expo_made"), sem("exp_done")
        decay_made, decay_rep = sem("decay_made"), sem("decay_rep")
        gate_made, gate_exp = sem("gate_made"), sem("gate_exp")
        gate_scanned = sem("gate_scanned")
        side_ready, side_turned = sem("side_ready"), sem("side_turned")
        side_act, side_acted = sem("side_act"), sem("side_acted")
        x_loaded = [sem(f"x_loaded{j}") for j in range(4)]
        x_used, out_made = sem("x_used"), sem("out_made")
        outs_stored = [sem(f"outs_stored{s}") for s in range(2)]
        pool_goes, act_goes, pe_goes = sem("pool_goes"), sem("act_goes"), sem("pe_goes")

        LANDS = 16 * K * PAIRS
        SMALL_LOADS = 3 * 3 + 4 + 8
        NORMS = [0, CHUNKS, 2 * CHUNKS, 3 * CHUNKS]
        STAGED = [k * (CHUNKS - 2) for k in (0, 1, 2, 3, 5)]
        FINALS = [final_d, final_s, final_d, final_s]
        NODE_ROWS = nodes[0:N, :]

        ctx.enter_context(nc.allow_non_contiguous_dma(reason="single numbers of the runs' ends"))
        block = ctx.enter_context(nc.Block())

        def bc_f(ap):
            return ap.unsqueeze(2).to_broadcast([P, K, D])

        def bc_t(ap):
            return ap.unsqueeze(1).to_broadcast([P, D, K])

        def tk(ap):
            return ap.rearrange("p (t f) -> p t f", f=D)

        def by_slot(ap):
            return ap.rearrange("p f t -> p t f")

        def by_feature(ap):
            return ap.rearrange("p t f -> p f t")

        def flat(ap):
            return ap.rearrange("p f t -> p (f t)")

        def cols(i, s):
            return bass.ds(i * (2 * K) + s * K, K)

        def fcols(i, s):
            return bass.ds(i * (2 * K * D) + s * K * D, K * D)

        def got_rows(s):
            return got[:, s, :].rearrange("p (t w) -> p t w", w=W)

        @block.sync
        def _(sp):
            def load_runs(array, dram, signal):
                a, b = runs(dram, EQ, ER)
                sp.dma_start(array[0:ER, 0:EQ + 1], a[:, :, 0]).then_inc(signal, 16)
                sp.dma_start(array[ER:P, 0:EQ], b[:, :, 0]).then_inc(signal, 16)
                sp.dma_start(array[ER:P, EQ:EQ + 1], b[:, EQ - 1:EQ, 0]).then_inc(signal, 16)

            def load_ends(ends, dram, signal):
                a, b = runs(dram, EQ, ER)
                sp.dma_start(ends[1:ER + 1, 0:1], a[:, EQ:EQ + 1, 0]).then_inc(signal, 16)
                sp.dma_start(ends[ER + 1:P, 0:1], b[0:P - ER - 1, EQ - 1:EQ, 0]).then_inc(signal, 16)
                sp.dma_start(ends[0:ER - 1, 1:2], a[1:ER, 0:1, 0]).then_inc(signal, 16)
                sp.dma_start(ends[ER - 1:P - 1, 1:2], b[:, 0:1, 0]).then_inc(signal, 16)

            load_runs(src_i, src, src_loaded)
            for array, dram in ((dst_i, dst), (wt, w), (w1t, w1)):
                load_runs(array, dram, loaded)
            sp.wait_ge(masks_set, 1)
            load_ends(ends_d, dst, loaded)
            sp.dma_start(wa_sb[:, :], Wa).then_inc(loaded, 16)
            sp.dma_start(WgWa[:, 0:D], Wg).then_inc(loaded, 16)
            sp.dma_start(WgWa[:, D:2 * D], Wa).then_inc(loaded, 16)
            for c in range(2):
                sp.dma_start(att[:, c:c + 1], att_w[c * D:(c + 1) * D, :]).then_inc(loaded, 16)
            sp.dma_start(dst_w[:, 1:2], gate_w[0:D, :]).then_inc(loaded, 16)
            sp.dma_start(src_w[:, 1:2], gate_w[2 * D:3 * D, :]).then_inc(loaded, 16)
            sp.dma_start(gmax_w[:, :], gate_w.rearrange("(a d) o -> a (d o)", d=D)[1:2, :].to_broadcast([P, D])).then_inc(loaded, 16)

            def copy_nodes(i, last=False):
                na, nb = (NQ + 1, NQ) if last else (4 * K * PAIRS, 4 * K * PAIRS)
                for a, b, n_ in zip(runs(x, NQ, NR), runs(NODE_ROWS, NQ, NR), (na, nb)):
                    m = min(4 * K, n_ - 4 * K * (PAIRS - 1))
                    sp.dma_start(b[:, bass.ds(i * (4 * K), m), :],
                                 a[:, bass.ds(i * (4 * K), m), :]).then_inc(nodes_copied, 16)

            sp.wait_ge(masks_set, 2)
            zeros = outrow[:, :, :].rearrange("p s a -> p (s a)")
            for table in (nodes, out):
                sp.dma_start(table[N:N + 2 * K * P, :].rearrange("(p t) d -> p (t d)", p=P),
                             zeros).then_inc(zeroed, 16)
                sp.dma_start(table[N + 2 * K * P:N + JUNK, :], zeros[:, 0:D]).then_inc(zeroed, 16)

            fa, fb = runs(attr, EQ, ER)
            filter_rows = filters.rearrange("(p t) w -> p (t w)", t=EC)

            def load_filter(i, s, last=False):
                na, nb = (EQ + 1 - (EC - K), EQ - (EC - K)) if last else (K, K)
                at = i * (2 * K) + s * K
                for v, lo, hi, m in ((fa, 0, ER, na), (fb, ER, P, nb)):
                    sp.dma_start(filter_in[lo:hi, s, 0:m, 0:D], v[:, bass.ds(at, m), :]).then_inc(filter_loaded[s], 16)

            def store_filter(i, s):
                sp.wait_ge(filter_named, i * 2 + (s + 1))
                sp.dma_start(filter_rows[:, bass.ds(i * (2 * K * W) + s * K * W, K * W)],
                             filter_in[:, s, :, :].rearrange("p t w -> p (t w)")).then_inc(filter_stored[s], 16)

            for s in range(2):
                load_filter(0, s)
            def filter_pairs(first, end):
                with sp.Fori(first, end) as i:
                    for s in range(2):
                        store_filter(i - 1, s)
                        sp.wait_ge(filter_stored[s], i * 16)
                        load_filter(i, s)
                    copy_nodes(i)

            copy_nodes(0)
            MID = min(PAIRS // 2 + 1, PAIRS - 1)
            filter_pairs(1, MID)
            sp.wait_ge(sort_done, 1)
            for dram, array in ((sorted_src, key[0]), (sorted_slot, tag[0])):
                sp.dma_start(dram.rearrange("(p t) o -> p (t o)", t=SC), array).then_inc(sort_stored, 16)
            sp.wait_ge(sort_stored, 32)
            load_runs(score_max[:, 1:1 + EC], sorted_src, sort_loaded)
            load_runs(gate_sum[:, 1:1 + EC], sorted_slot, sort_loaded)
            load_ends(ends_s, sorted_src[0:E, :], sort_loaded)
            if MID < PAIRS - 1:
                filter_pairs(MID, PAIRS - 1)
            for s in range(2):
                store_filter(PAIRS - 2, s)
                sp.wait_ge(filter_stored[s], (PAIRS - 1) * 16)
                load_filter(PAIRS - 1, s, last=(s == 1))
            copy_nodes(PAIRS - 1, last=True)
            for s in range(2):
                store_filter(PAIRS - 1, s)

            for s in range(2):
                sp.wait_ge(scattered[s], 3 * LANDS)
            sp.wait_ge(side_scattered, 48)
            xa, xb = runs(NODE_ROWS, NQ, NR)
            oa, ob = runs(out[0:N, :], NQ, NR)

            def tile_io(i, j, views, tile, load, signal, last):
                na, nb = (NQ + 1 - K * (TILES - 1), NQ - K * (TILES - 1)) if last else (K, K)
                at = i * (4 * K) + j * K
                for v, lo, hi, m in ((views[0], 0, NR, na), (views[1], NR, P, nb)):
                    dram, on_chip = v[:, bass.ds(at, m), :], tk(tile)[lo:hi, 0:m, :]
                    if load:
                        sp.dma_start(on_chip, dram).then_inc(signal, 16)
                    else:
                        sp.dma_start(dram, on_chip).then_inc(signal, 16)

            def load_x(i, j, start, last):
                if not start:
                    sp.wait_ge(x_used, i * 4 + (j - 3))
                tile_io(i, j, (xa, xb), rowin[:, j * K * D:(j + 1) * K * D], True, x_loaded[j], last)

            def store_tile(i, j, last=False):
                sp.wait_ge(out_made, i * 4 + (j + 1))
                tile_io(i, j, (oa, ob), outrow[:, j % 2, :], False, outs_stored[j % 2], last)

            def node_tiles(i, start=False, last=False):
                for j in range(4):
                    load_x(i, j, start, last and j == 3)
                    if j == 3:
                        store_tile(i, 0)
                    elif not start:
                        store_tile(i - 1, j + 1)

            node_tiles(0, start=True)
            with sp.Fori(1, PAIRS - 1) as i:
                node_tiles(i)
            node_tiles(PAIRS - 1, last=True)
            for j in (1, 2, 3):
                store_tile(PAIRS - 1, j, last=(j == 3))
            for s in range(2):
                sp.wait_ge(outs_stored[s], 16 * TILES)
                sp.wait_ge(scattered[s], 4 * LANDS)
            sp.wait_ge(side_scattered, 64)

        @block.gpsimd
        def _(pool):
            junk_i = gate_sum[:, 1:1 + EC].bitcast(I32)
            slot_i = weight_sum[:, 1:1 + EC].bitcast(I32)
            nc.gpsimd.iota(pidx_i[:, :], pattern=[[0, 1]], base=0, channel_multiplier=1).then_inc(consts, 1)
            nc.gpsimd.iota(junk_i, pattern=[[0, PAIRS], [P, 2 * K]], base=N, channel_multiplier=1).then_inc(consts, 1)
            nc.gpsimd.iota(slot_i, pattern=[[1, EC]], base=0, channel_multiplier=EC).then_inc(consts, 1)
            nc.gpsimd.memset(ident[:, :], 0.0).then_inc(consts, 1)
            nc.gpsimd.memset(real[:, 0:EQ + 1], 1.0).then_inc(consts, 1)
            nc.gpsimd.memset(real[:, EQ + 1:EC], 0.0).then_inc(consts, 1)
            pool.wait_ge(consts, 6)
            nc.gpsimd.affine_select(out=ident[:, :], in_=ident[:, :], compare_op=ALU.not_equal, fill=1.0,
                                    base=0, pattern=[[-1, P]], channel_multiplier=1).then_inc(consts, 1)
            nc.gpsimd.affine_select(out=real[:, EQ:EQ + 1], in_=real[:, EQ:EQ + 1], compare_op=ALU.is_ge,
                                    fill=0.0, base=ER - 1, pattern=[[0, 1]],
                                    channel_multiplier=-1).then_inc(consts, 1)
            copies = Count()

            def stage_copy(to, array, i, s):
                nc.gpsimd.tensor_copy(to[:, s, :], array[:, cols(i, s)]).then_inc(staged, copies.up())

            def chunk(n, i, s, free_at, streams):
                pool.wait_ge(got_free, i * 2 + (free_at + s + 1))
                if len(streams) == 2:
                    pool.wait_ge(got_dst_free, i * 2 + (s + 1))
                pool.wait_ge(staged, copies.now())
                if not (isinstance(i, int) and i == 0):
                    m = len(streams)
                    pool.wait_ge(next_staged, i * (2 * m) + (STAGED[n] + 2 + (s - 1) * m))
                pool.sem_inc(pool_goes, 1)
                for t in range(K):
                    for to, from_, width, indices, _, signal in streams:
                        nc.gpsimd.indirect_dma_start(
                            out=to[:, s, t * width:(t + 1) * width], out_offset=None, in_=from_,
                            in_offset=bass.IndirectOffsetOnAxis(ap=indices[:, s, t:t + 1], axis=0),
                        ).then_inc(signal[s], 16)

            def gather_pass(n, free_at, streams):
                for s in range(2):
                    for k, (_, _, _, indices, array, signal) in enumerate(streams):
                        if n and not k:
                            pool.wait_ge(signal[s], n * LANDS)
                            pool.wait_ge(scattered[s], SCATTERED[n])
                        stage_copy(indices, array, 0, s)
                chunk(n, 0, 0, free_at, streams)
                with pool.Fori(0, PAIRS - 1) as i:
                    chunk(n, i, 1, free_at, streams)
                    chunk(n, i + 1, 0, free_at, streams)
                chunk(n, PAIRS - 1, 1, free_at, streams)
                for s in range(2):
                    pool.wait_ge(landed[s], (n + 1) * LANDS)
                    if len(streams) == 2:
                        pool.wait_ge(landed_dst[s], LANDS)

            SCATTERED = [0, LANDS, LANDS, 2 * LANDS, 3 * LANDS]

            def scatter_pass(n, side, to):
                def free_slot(i, s):
                    pool.wait_ge(scattered[s], i * (16 * K) + n * LANDS)
                    pool.sem_inc(outrow_free, 1)

                def scatter(i, s, then=None):
                    pool.wait_ge(out_staged, i * 2 + (n * CHUNKS + s + 1))
                    pool.wait_ge(outrow_made, i * 2 + (n * CHUNKS + s + 1))
                    pool.sem_inc(pool_goes, 1)
                    for t in range(K):
                        if t == K // 2 and then:
                            then()
                        nc.gpsimd.indirect_dma_start(
                            out=to, out_offset=bass.IndirectOffsetOnAxis(ap=stage_out[:, s, t:t + 1], axis=0),
                            in_=outrow[:, s, t * D:(t + 1) * D], in_offset=None,
                            compute_op=ALU.add).then_inc(scattered[s], 16)

                scatter(0, 0)
                with pool.Fori(0, PAIRS - 1) as i:
                    scatter(i, 1, lambda: free_slot(i + 1, 0))
                    scatter(i + 1, 0, lambda: free_slot(i + 1, 1))
                scatter(PAIRS - 1, 1)
                pool.wait_ge(side_made, n + 1)
                nc.gpsimd.indirect_dma_start(
                    out=to, out_offset=bass.IndirectOffsetOnAxis(ap=side[:, 0:1], axis=0),
                    in_=side_out[:, :], in_offset=None, compute_op=ALU.add).then_inc(side_scattered, 16)
                for s in range(2):
                    pool.wait_ge(scattered[s], (n + 1) * LANDS)
                pool.wait_ge(side_scattered, 16 * (n + 1))
                pool.sem_inc(outrow_free, 2)

            pool.wait_ge(src_ready, 1)
            gather_pass(0, 0, [(got, x, D, stage, src_i, landed)])
            pool.wait_ge(nodes_copied, 32 * PAIRS)
            pool.wait_ge(zeroed, 64)
            pool.wait_ge(ready_s, 1)
            scatter_pass(0, side_final_d, nodes)
            for s in range(2):
                pool.wait_ge(filter_stored[s], 16 * PAIRS)
            gather_pass(1, CHUNKS, [(got, filters, W, stage, slot_s, landed)])
            pool.wait_ge(got_free, 2 + 2 * CHUNKS)
            gather_pass(2, 2 * CHUNKS, [(got, NODE_ROWS, D, stage, dst_s, landed)])
            scatter_pass(1, side_final_s, nodes)
            gather_pass(3, 3 * CHUNKS, [(got, NODE_ROWS, D, stage, src_i, landed),
                                        (got_dst, NODE_ROWS, D, stage_dst, dst_i, landed_dst)])
            scatter_pass(2, side_final_d, nodes)
            gather_pass(4, 4 * CHUNKS, [(got, NODE_ROWS, D, stage, dst_s, landed)])
            for s in range(2):
                pool.wait_ge(outs_stored[s], 16 * TILES)
            scatter_pass(3, side_final_s, out)

        @block.scalar
        def _(act):
            def deviation_of(n, s):
                act.wait_ge(summed, n)
                nc.scalar.activation(std[:, s, :], sumsq[:, s, :], ACT.Sqrt, bias=eps[:, 0:1],
                                     scale=1.0 / D).then_inc(deviated, 1)

            def stage_next(n, i, s, streams):
                for k, (to, array) in enumerate(streams):
                    act.wait_ge((landed_dst if k else landed)[s], i * (16 * K) + ((0 if k else n * LANDS) + 16 * K))
                    nc.scalar.activation(to[:, s, :], array[:, cols(i + 1, s)], ACT.Copy).then_inc(next_staged, 1)

            act.wait_ge(loaded, 16 * SMALL_LOADS)
            act.wait_ge(ready_d, 1)
            def take_rows(i, s, last=False):
                act.wait_ge(landed[s], i * (16 * K) + 16 * K)
                nc.scalar.activation(kept[:, fcols(i, s)], got[:, s, 0:K * D], ACT.Copy).then_inc(got_free, 1)
                if not last:
                    stage_next(0, i, s, [(stage, src_i)])
                act.wait_ge(filter_loaded[s], i * 32 + 32)
                nc.scalar.activation(filter_in[:, s, :, D], dst_i[:, cols(i, s)],
                                     ACT.Copy).then_inc(filter_named, 1)

            with act.Fori(0, PAIRS - 1) as i:
                for s in range(2):
                    take_rows(i, s)

            def make_mask(array, i, s, n):
                act.wait_ge(scanned, n)
                nc.scalar.activation(mask_rep[:, s, :, 1:K + 1], bc_t(array[:, cols(i, s)]),
                                     ACT.Copy).then_inc(mask_made, 1)

            def keep_sums(layer, i, s):
                act.wait_ge(scanned, i * 2 + (layer * CHUNKS + s + 3))
                nc.scalar.activation(tk(kept[:, fcols(i, s)]), by_slot(run[:, s, :, 1:K + 1]),
                                     ACT.Copy).then_inc(sums_kept, 1)

            def fill_outrow(n, i, s):
                act.wait_ge(outrow_free, i * 2 + (n * CHUNKS + s + 1))
                act.sem_inc(act_goes, 1)
                nc.scalar.activation(stage_out[:, s, :], FINALS[n][:, cols(i, s)], ACT.Copy).then_inc(out_staged, 1)
                nc.scalar.activation(outrow[:, s, :], kept[:, fcols(i, s)], ACT.Copy).then_inc(outrow_made, 1)

            def chunk_of(layer, i, s, last=False):
                if not (last and s == 1):
                    ni, ns = (i, 1) if s == 0 else (i + 1, 0)
                    make_mask(SAMES[layer], ni, ns, i * 2 + (layer * CHUNKS + s + 2))
                deviation_of(i * 2 + (NORMS[layer] + s + 1), s)
                if layer and not last:
                    stage_next(2, i, s, [(stage, dst_s)])
                keep_sums(layer, i, s)
                if layer == 0:
                    act.wait_ge(sums_kept, i * 2 + (s + 3))
                    fill_outrow(0, i, s)

            SAMES = [same_d, same_s]
            for layer, same in enumerate(SAMES):
                if layer == 0:
                    act.wait_ge(sort_done, 2)
                    act.wait_ge(zeroed, 64)
                    make_mask(same, 0, 0, 1)
                    for s in range(2):
                        chunk_of(0, 0, s)
                    for s in range(2):
                        take_rows(PAIRS - 1, s, last=True)
                else:
                    act.wait_ge(ready_s, 1)
                    def take_filters(i, s, last=False):
                        act.wait_ge(landed[s], i * (16 * K) + (LANDS + 16 * K))
                        nc.scalar.activation(dst_s[:, cols(i, s)], got_rows(s)[:, :, D], ACT.Copy)
                        nc.scalar.activation(tk(kept[:, fcols(i, s)]), got_rows(s)[:, :, 0:D],
                                             ACT.Copy).then_inc(got_free, 1)
                        if not last:
                            stage_next(1, i, s, [(stage, slot_s)])

                    with act.Fori(0, PAIRS - 1) as i:
                        for s in range(2):
                            take_filters(i, s)
                    for s in range(2):
                        take_filters(PAIRS - 1, s, last=True)
                    make_mask(same, 0, 0, CHUNKS + 1)
                with act.Fori(1 - layer, PAIRS - 1) as i:
                    for s in range(2):
                        chunk_of(layer, i, s)
                if layer:
                    act.wait_ge(sums_kept, 2 * CHUNKS)
                    for s in range(2):
                        fill_outrow(1, 0, s)
                for s in range(2):
                    chunk_of(layer, PAIRS - 1, s, last=True)
            act.wait_ge(sums_kept, 2 * CHUNKS + 2)
            with act.Fori(1, PAIRS) as i:
                for s in range(2):
                    fill_outrow(1, i, s)

            def deviations(g):
                act.wait_ge(summed, g + (NORMS[2] + 1))
                nc.scalar.activation(std[:, 0:2, :], sumsq[:, 0:2, :], ACT.Sqrt, bias=eps[:, 0:1],
                                     scale=1.0 / D).then_inc(deviated, 1)

            def keep_turned(g):
                for side in range(2):
                    for q, (t0, nt) in enumerate(GROUPS):
                        act.wait_ge(turned, g * 8 + (4 * side + q + 1))
                        nc.scalar.activation(hT[:, side, t0 * P:(t0 + nt) * P],
                                             hT_ps[0:D, q % 2, 0:nt * P], ACT.Copy).then_inc(turned_free, 1)

            def exps(g, s):
                act.wait_ge(expo_made, g + 1)
                nc.scalar.activation(wexp[:, s, :, :], expo[:, :, :], ACT.Exp).then_inc(exp_done, 1)
                act.wait_ge(decay_made, g + 1)
                act.wait_ge(scanned, g + (2 * CHUNKS + 2))
                nc.scalar.activation(mask_rep[:, 0, :, 1:K + 1], bc_t(decay[:, s, :]),
                                     ACT.Copy).then_inc(decay_rep, 1)

            def caps(i, s):
                act.wait_ge(gate_scanned, i * 2 + (s + 1))
                nc.scalar.activation(mask_rep[:, 1, :, 1:K + 1], bc_t(cap[:, cols(i, s)]),
                                     ACT.Copy).then_inc(mask_made, 1)

            BOTH = [(stage, src_i), (stage_dst, dst_i)]

            def attend(i, s, more, more2, more4=False, fills=()):
                g = i * 2 + s
                if more2:
                    deviations(g + 2)
                if more4:
                    stage_next(3, i + 1, s, BOTH)
                caps(i, s)
                for f in fills[0:1]:
                    fill_outrow(2, *f)
                if more:
                    keep_turned(g + 1)
                for f in fills[1:2]:
                    fill_outrow(2, *f)
                act.wait_ge(gate_made, g + 1)
                nc.scalar.activation(gexp[:, :], gate[:, :], ACT.Exp, scale=-1.0).then_inc(gate_exp, 1)
                if more:
                    exps(g + 1, 1 - s)

            act.wait_ge(masks_set, 3)
            for s in range(2):
                deviations(s)
                stage_next(3, 0, s, BOTH)
            keep_turned(0)
            exps(0, 0)
            with act.Fori(0, PAIRS - 2) as i:
                for s in range(2):
                    attend(i, s, True, True, True)
            act.wait_ge(kept_made, 2)
            for s in range(2):
                fill_outrow(2, 0, s)
            early = [[(q, 0), (q, 1)] if 2 * q + 1 <= CHUNKS - 6 else [] for q in (1, 2, 3)]
            rest = 1 + sum(1 for q in early if q)
            act.wait_ge(kept_made, 2 * rest)
            attend(PAIRS - 2, 0, True, True)
            attend(PAIRS - 2, 1, True, True, fills=early[0])
            attend(PAIRS - 1, 0, True, False, fills=early[1])
            attend(PAIRS - 1, 1, False, False, fills=early[2])
            act.wait_ge(kept_made, CHUNKS)

            def fill_pairs(first, end):
                if first < end:
                    with act.Fori(first, end) as i:
                        for s in range(2):
                            fill_outrow(2, i, s)

            halfway = min(PAIRS, max(rest, PAIRS // 2 + 2))
            fill_pairs(rest, halfway)
            act.wait_ge(side_act, 1)
            nc.scalar.activation(wexpT, expT, ACT.Exp).then_inc(side_acted, 1)
            act.wait_ge(side_act, 2)
            nc.scalar.activation(side_s[:, 10:12], side_s[:, 8:10], ACT.Exp).then_inc(side_acted, 1)
            act.wait_ge(side_act, 3)
            nc.scalar.activation(side_s[:, 15:16], side_s[:, 14:15], ACT.Exp, scale=-1.0).then_inc(side_acted, 1)
            fill_pairs(halfway, PAIRS)

            def square_of(g, s):
                act.wait_ge(centered, g + 1)
                nc.scalar.activation(square[:, s, :], center[:, s, :], ACT.Square).then_inc(squared, 1)

            def rows_of(i, j):
                act.wait_ge(shifted, i * 2 + (j // 2 + 1))
                for t in range(K):
                    at = (j * K + t) * D
                    m = nc.scalar.activation(hrow[:, j % 2, t * D:(t + 1) * D], rowin[:, at:at + D], ACT.Relu,
                                             bias=shift[:, j % 2, t:t + 1], scale=rstd[:, j % 2, t:t + 1])
                m.then_inc(rows_made, 1)

            def half(i, s, last=False, more=True):
                if not last:
                    for j in (2 * s, 2 * s + 1):
                        rows_of(i, j)
                    deviation_of(i * 4 + (NORMS[3] + 2 * s + 3), slice(0, 2))
                keep_sums(3, i, s)
                if not last:
                    ni, ns = (i, 1) if s == 0 else (i + 1, 0)
                    make_mask(same_s, ni, ns, i * 2 + (3 * CHUNKS + s + 2))
                    if isinstance(i, int) and i == PAIRS - 1:
                        rows_of(i, 2)
                    square_of(i * 2 + (s + 1), ns)
                    deviation_of(i * 4 + (NORMS[3] + 2 * s + 4), 2 + ns)
                    if isinstance(i, int) and i == PAIRS - 1:
                        rows_of(i, 3)
                    if more:
                        stage_next(4, ni, ns, [(stage, dst_s)])

            act.wait_ge(masks_set, 4)
            make_mask(same_s, 0, 0, 3 * CHUNKS + 1)
            deviation_of(NORMS[3] + 1, slice(0, 2))
            square_of(0, 0)
            deviation_of(NORMS[3] + 2, 2)
            stage_next(4, 0, 0, [(stage, dst_s)])
            with act.Fori(0, PAIRS - 2) as i:
                for s in range(2):
                    half(i, s)
            half(PAIRS - 2, 0)
            half(PAIRS - 2, 1, more=False)
            half(PAIRS - 1, 0, more=False)
            half(PAIRS - 1, 1, last=True)

        @block.tensor
        def _(pe):
            pe.wait_ge(loaded, 16 * SMALL_LOADS)
            pe.wait_ge(consts, 8)
            nc.tensor.transpose(side_ps[0:D, 0:D], wa_sb[:, :], ident[0:D, 0:D]).then_inc(side_turned, 1)
            pe.wait_ge(side_ready, 1)
            nc.tensor.matmul(side_ps[0:D, 0:2], waT[:, :], att[:, :], start=True, stop=True).then_inc(side_turned, 1)

            def turn_tails(n, counts):
                pe.wait_ge(side_ready, n)
                for c in range(counts):
                    m = nc.tensor.transpose(side_ps[0:W, c * P:(c + 1) * P], tails[:, c, :], ident[:, :])
                m.then_inc(side_turned, 1)

            def turn_back(n, counts):
                pe.wait_ge(side_ready, n)
                for c in range(counts):
                    m = nc.tensor.transpose(side_ps[:, c * P:c * P + W], inT[:, c, :], ident[0:W, 0:W])
                m.then_inc(side_turned, 1)

            for layer in range(2):
                turn_tails(2 + 3 * layer, 2)
                turn_tails(3 + 3 * layer, 1)
                turn_back(4 + 3 * layer, 1)
            turn_tails(8, 2)

            def turn_group(g, side, q):
                t0, nt = GROUPS[q]
                pe.wait_ge(turned_free, g * 8 + (4 * side + q + 1))
                pe.sem_inc(pe_goes, 1)
                rows = tk(hrow[:, side, :])
                for t in range(nt):
                    m = nc.tensor.transpose(hT_ps[0:D, q % 2, t * P:(t + 1) * P], rows[:, t0 + t, :], ident[:, :])
                m.then_inc(turned, 1)

            def shares(g, side, q, weights):
                t0, nt = GROUPS[q]
                pe.wait_ge(turned_free, g * 8 + (4 * side + q + 3))
                for t in range(t0, t0 + nt):
                    at = side * 2 * K + 2 * t
                    m = nc.tensor.matmul(share_ps[:, at:at + 2], hT[:, side, t * P:(t + 1) * P],
                                         weights[:, :], start=True, stop=True)
                if side == 1 and q == 3:
                    m.then_inc(shares_made, 1)

            def heads(g):
                pe.wait_ge(shares_used, g + 1)
                for side, weights in ((0, src_w), (1, dst_w)):
                    pe.wait_ge(hrow_made, g * 2 + (side + 1))
                    for q in range(4):
                        turn_group(g, side, q)
                        if q:
                            shares(g, side, q - 1, weights)
                    shares(g, side, 3, weights)
                pe.wait_ge(feat_free, g + 1)
                pe.wait_ge(value_free, g + 1)
                for t in range(K):
                    for c, to in enumerate((feat_ps, value_ps)):
                        m = nc.tensor.matmul(to[:, t * D:(t + 1) * D], hT[:, 0, t * P:(t + 1) * P],
                                             WgWa[:, c * D:(c + 1) * D], start=True, stop=True)
                m.then_inc(proj_made, 1)

            pe.wait_ge(masks_set, 3)
            with pe.Fori(0, PAIRS) as i:
                for s in range(2):
                    heads(i * 2 + s)
            turn_tails(9, 4)
            turn_back(10, 4)
            turn_tails(11, 2)
            turn_tails(12, 2)
            turn_back(13, 2)

        @block.vector
        def _(dve):
            n = Count()
            V = nc.vector

            def settle():
                dve.wait_ge(dve_step, n.now())

            def op(f, *a, **k):
                dve.wait_ge(dve_step, n.now())
                return f(*a, **k).then_inc(dve_step, n.up())

            V.memset(ends_d[:, :], -1).then_inc(dve_step, n.up())
            V.memset(ends_s[:, :], -1.0).then_inc(dve_step, n.up())
            settle()
            dve.sem_inc(masks_set, 1)
            dve.wait_ge(src_loaded, 48)
            for c in range(EQ + 1, EC):
                op(V.tensor_copy, src_i[:, c:c + 1], src_i[:, c - 1:c])
            settle()
            dve.sem_inc(src_ready, 1)
            dve.sem_inc(got_free, 2)
            dve.sem_inc(next_staged, 2)

            V.memset(eps[:, :], EPS).then_inc(dve_step, n.up())
            V.memset(outrow[:, :, :], 0.0).then_inc(dve_step, n.up())
            V.memset(run[:, :, :, :], 0.0).then_inc(dve_step, n.up())
            V.memset(filter_in, 0.0).then_inc(dve_step, n.up())
            for row in (side_sum, side_max):
                V.memset(row[:, :], 0.0).then_inc(dve_step, n.up())
            for array in (score_max, gate_sum, weight_sum):
                V.memset(array[:, 0:1], 0.0).then_inc(dve_step, n.up())
            settle()
            dve.sem_inc(masks_set, 1)
            for s_, free in ((scanned, 2), (sums_kept, 2), (got_dst_free, 2),
                             (outrow_free, 2), (turned_free, 2), (shares_used, 1), (feat_free, 1),
                             (value_free, 1), (gate_scanned, 1)):
                dve.sem_inc(s_, free)

            dve.wait_ge(loaded, 16 * SMALL_LOADS)
            dve.wait_ge(consts, 8)
            for c in range(EQ + 1, EC):
                for array in (dst_i, wt, w1t):
                    op(V.tensor_copy, array[:, c:c + 1], array[:, c - 1:c])
            settle()
            dve.sem_inc(ready_d, 1)
            op(V.tensor_tensor, wt[:, :], wt[:, :], real[:, :], ALU.mult)
            op(V.tensor_copy, pidx[:, :], pidx_i[:, :])
            junk = rdeg[:, :]
            op(V.tensor_copy, junk, gate_sum[:, 1:1 + EC].bitcast(I32))
            op(V.tensor_copy, tag[0][:, 0:EC], weight_sum[:, 1:1 + EC].bitcast(I32))

            for b in range(7):
                op(V.tensor_scalar, pbit_i[:, b:b + 1], pidx_i[:, :], b, None, ALU.logical_shift_right)
            op(V.tensor_scalar, pbit_i[:, 0:7], pbit_i[:, 0:7], 1, None, ALU.bitwise_and)
            op(V.tensor_copy, pbit[:, 0:7], pbit_i[:, 0:7])
            op(V.tensor_scalar, tmp[:, 0:1], pbit[:, 5:6], float(32 * EC), None, ALU.mult)
            op(V.tensor_scalar, tmp[:, 1:2], pbit[:, 6:7], float(64 * EC), None, ALU.mult)
            op(V.tensor_tensor, tmp[:, 0:1], tmp[:, 0:1], tmp[:, 1:2], ALU.add)
            op(V.tensor_scalar, pbit[:, 0:7], pbit[:, 0:7], -2.0, 1.0, ALU.mult, ALU.add)
            op(V.tensor_scalar, tag[1].bitcast(I32)[:, 0:EC], tag[0][:, 0:EC], tmp[:, 0:1], None, ALU.subtract)
            h_i = word.bitcast(I32)
            op(V.memset, h_i[:, EC:SC], FILL + BIAS)
            op(V.memset, tag[1].bitcast(I32)[:, EC:SC], 0)
            op(V.tensor_scalar, key[0][:, 0:EC], src_i[:, :], float(-FILL), None, ALU.add)
            op(V.tensor_tensor, key[0][:, 0:EC], key[0][:, 0:EC], real[:, :], ALU.mult)
            op(V.tensor_scalar, h_i[:, 0:EC], key[0][:, 0:EC], float(FILL + BIAS), None, ALU.add)
            op(V.tensor_scalar, h_i, h_i, LOWBITS, None, ALU.logical_shift_left)
            op(V.tensor_tensor, key[0].bitcast(I32), h_i, tag[1].bitcast(I32), ALU.bitwise_or)

            at = [0]

            def turn_blocks():
                a, b = at[0], 1 - at[0]
                op(V.transpose, key[b], key[a])
                if tagged[0]:
                    op(V.transpose, tag[b], tag[a])
                at[0] = b

            tagged = [False]

            def parts(array, j):
                v = array.rearrange("p (b h l) -> p b h l", h=2, l=1 << j)
                return v[:, :, 0, :], v[:, :, 1, :]

            def exchange(views_a, views_b, tags_a, tags_b):
                (lo, hi), (to_lo, to_hi) = views_a, views_b
                if tagged[0]:
                    (tlo, thi), (to_tlo, to_thi) = tags_a, tags_b
                    m, d = like(swap, lo), like(diff, lo)
                    op(V.tensor_tensor, m, lo, hi, ALU.is_gt)
                    V.tensor_tensor(d, thi, tlo, ALU.subtract).then_inc(dve_step, n.up())
                    op(V.tensor_tensor, d, d, m, ALU.mult)
                    op(V.tensor_tensor, to_tlo, tlo, d, ALU.add)
                    V.tensor_tensor(to_thi, thi, d, ALU.subtract).then_inc(dve_step, n.up())
                else:
                    settle()
                V.tensor_tensor(to_lo, lo, hi, ALU.min).then_inc(dve_step, n.up())
                V.tensor_tensor(to_hi, lo, hi, ALU.max).then_inc(dve_step, n.up())

            def like(array, view):
                shape = view.shape
                if len(shape) == 3:
                    return array.rearrange("p (b l) -> p b l", l=shape[2])
                return array

            def column_stage(j):
                a, b = at[0], 1 - at[0]
                exchange(parts(key[a], j), parts(key[b], j), parts(tag[a], j), parts(tag[b], j))
                at[0] = b

            def flip(bit):
                k_ = key[at[0]]
                if bit < 9:
                    hi = parts(k_, bit)[1]
                    op(V.tensor_scalar, hi, hi, -1.0, None, ALU.mult)
                elif bit < 16:
                    op(V.tensor_scalar, k_, k_, pbit[:, bit - 9:bit - 8], None, ALU.mult)

            def far_stage(j):
                a, b = at[0], 1 - at[0]
                far = 1 << (j - 9)
                for base in range(0, P, 2 * far):
                    for low in range(base, base + far, 32):
                        high = low + far
                        L, H = slice(low, low + 32), slice(high, high + 32)
                        op(V.tensor_copy, kh[L, :], key[a][H, :])
                        V.tensor_copy(th[L, :], tag[a][H, :]).then_inc(dve_step, n.up())
                        op(V.tensor_tensor, mk[L, :], key[a][L, :], kh[L, :], ALU.is_gt)
                        V.tensor_tensor(df[L, :], th[L, :], tag[a][L, :], ALU.subtract).then_inc(dve_step, n.up())
                        V.tensor_tensor(key[b][L, :], key[a][L, :], kh[L, :], ALU.min).then_inc(dve_step, n.up())
                        V.tensor_tensor(key[b][H, :], key[a][L, :], kh[L, :], ALU.max).then_inc(dve_step, n.up())
                        op(V.tensor_tensor, df[L, :], df[L, :], mk[L, :], ALU.mult)
                        op(V.tensor_tensor, tag[b][L, :], tag[a][L, :], df[L, :], ALU.add)
                        V.tensor_tensor(tag[b][H, :], th[L, :], df[L, :], ALU.subtract).then_inc(dve_step, n.up())
                settle()
                at[0] = b

            spare = center[:, :, :].rearrange("p s a -> p (s a)")
            kh, th = spare[:, 0:SC], spare[:, SC:2 * SC]
            mk, df = spare[:, 2 * SC:3 * SC], word

            for phase in range(1, 17):
                if phase == 15:
                    a, b = at[0], 1 - at[0]
                    op(V.tensor_scalar, key[a], key[a], pbit[:, 5:6], None, ALU.mult)
                    op(V.tensor_scalar, h_i, key[a].bitcast(I32), (1 << LOWBITS) - 1, None, ALU.bitwise_and)
                    op(V.tensor_scalar, tag[b], h_i, tmp[:, 0:1], None, ALU.add)
                    op(V.tensor_scalar, h_i, key[a].bitcast(I32), LOWBITS, None, ALU.logical_shift_right)
                    op(V.tensor_scalar, key[b], h_i, float(-BIAS), None, ALU.add)
                    tagged[0] = True
                    at[0] = b
                    flip(15)
                else:
                    if phase > 1:
                        flip(phase - 1)
                    flip(phase)
                for j in range(phase - 1, 13, -1):
                    far_stage(j)
                if phase > 9:
                    turn_blocks()
                    for j in range(min(phase - 1, 13), 8, -1):
                        column_stage(j - 9)
                    turn_blocks()
                for j in range(min(phase - 1, 8), -1, -1):
                    column_stage(j)
            if at[0]:
                op(V.tensor_copy, key[0], key[1])
                op(V.tensor_copy, tag[0], tag[1])
            settle()
            dve.sem_inc(sort_done, 1)

            def make_order(d, end, same, pick, final, cont, side_final, jk):
                e, f, r = same, pick, for_counts
                op(V.tensor_scalar, f[:, :], d, d[:, 0:1], None, ALU.is_equal)
                op(V.tensor_tensor, cont[:, 1:2], d[:, 0:1], end[:, 0:1], ALU.is_equal)
                op(V.tensor_tensor, notn[:, :], d[:, EC - 1:EC], end[:, 1:2], ALU.not_equal)
                op(V.tensor_tensor, cont[:, 0:1], f[:, EC - 1:EC], cont[:, 1:2], ALU.mult)
                op(V.tensor_scalar, tmp[:, 2:3], notn[:, :], -1.0, 1.0, ALU.mult, ALU.add)
                op(V.tensor_tensor, tmp[:, 2:3], tmp[:, 2:3], f[:, EC - 1:EC], ALU.mult)
                op(V.tensor_scalar, tmp[:, 2:3], tmp[:, 2:3], -1.0, 1.0, ALU.mult, ALU.add)
                op(V.tensor_scalar, tmp[:, 3:4], pidx[:, :], float(N + 2 * K * P), None, ALU.add)
                op(V.tensor_tensor, tmp[:, 1:2], d[:, 0:1], tmp[:, 3:4], ALU.subtract)
                op(V.tensor_tensor, tmp[:, 1:2], tmp[:, 1:2], tmp[:, 2:3], ALU.mult)
                op(V.tensor_tensor, side_final[:, :], tmp[:, 1:2], tmp[:, 3:4], ALU.add)
                op(V.tensor_tensor, e[:, 0:EC - 1], d[:, 0:EC - 1], d[:, 1:EC], ALU.not_equal)
                op(V.memset, e[:, EC - 1:EC], 1.0)
                op(V.tensor_tensor, pick[:, :], f[:, :], e[:, :], ALU.mult)
                op(V.tensor_tensor, r, e[:, :], pick[:, :], ALU.subtract)
                op(V.tensor_tensor, r[:, EC - 1:EC], r[:, EC - 1:EC], notn[:, :], ALU.mult)
                op(V.memset, same[:, 0:1], 0.0)
                op(V.tensor_tensor, same[:, 1:EC], d[:, 1:EC], d[:, 0:EC - 1], ALU.is_equal)
                op(V.tensor_tensor, d, d, jk, ALU.subtract)
                op(V.tensor_tensor, d, d, r, ALU.mult)
                op(V.tensor_tensor, final[:, :], d, jk, ALU.add)

            d = weight_sum[:, 1:1 + EC]
            op(V.tensor_copy, d, dst_i[:, :])
            op(V.tensor_copy, endf[:, :], ends_d[:, :])
            make_order(d, endf, same_d, pick_d, final_d, cont_d, side_final_d, junk)
            dve.wait_ge(sort_loaded, 16 * 10)
            for c in range(EQ + 1, EC):
                for array in (score_max, gate_sum):
                    op(V.tensor_copy, array[:, 1 + c:2 + c], array[:, c:1 + c])
            op(V.tensor_copy, slot_s[:, :], gate_sum[:, 1:1 + EC])
            make_order(score_max[:, 1:1 + EC], ends_s, same_s, pick_s, final_s, cont_s, side_final_s, junk)
            settle()
            dve.sem_inc(ready_s, 1)
            op(V.memset, mask_rep[:, :, :, :], 0.0)
            op(V.memset, msg[:, :, :, :], 0.0)
            settle()
            dve.sem_inc(sort_done, 1)
            dve.wait_ge(side_turned, 1)
            V.tensor_copy(waT[:, :], side_ps[0:D, 0:D]).then_inc(side_ready, 1)
            dve.wait_ge(side_turned, 2)
            op(V.tensor_copy, src_w[:, 0:1], side_ps[0:D, 0:1])
            op(V.tensor_copy, dst_w[:, 0:1], side_ps[0:D, 1:2])

            def turn_masks(cont, turned_at):
                op(V.tensor_copy, tails[:, 0, :], cont[:, 0:1].to_broadcast([P, W]))
                op(V.tensor_copy, tails[:, 1, :], cont[:, 1:2].to_broadcast([P, W]))
                settle()
                dve.sem_inc(side_ready, 1)
                dve.wait_ge(side_turned, turned_at)
                op(V.tensor_copy, maskT[:, 0, :], side_ps[0:W, 0:P])
                op(V.tensor_copy, maskT[:, 1, :], side_ps[0:W, P:2 * P])

            def carry_sums(turned_at, tail, counts=None):
                op(V.memset, tails[:, 0, D:W], 0.0)
                op(V.memset, chainT[:, :, 0:1], 0.0)
                op(V.tensor_copy, tails[:, 0, 0:D], tail)
                if counts is not None:
                    op(V.memset, tails[:, 1, :], 0.0)
                    op(V.tensor_copy, tails[:, 1, 0:1], counts)
                settle()
                dve.sem_inc(side_ready, 1)
                dve.wait_ge(side_turned, turned_at)
                for c in range(1 if counts is None else 2):
                    op(V.tensor_tensor_scan, chainT[:, c, 1:P + 1], maskT[:, 0, :],
                       side_ps[0:W, c * P:(c + 1) * P], 0.0, ALU.mult, ALU.add)
                    op(V.tensor_tensor, inT[:, c, :], chainT[:, c, 0:P], maskT[:, 1, :], ALU.mult)
                settle()
                dve.sem_inc(side_ready, 1)
                dve.wait_ge(side_turned, turned_at + 1)

            def degrees(same, pick):
                deg = weight_sum[:, 1:1 + EC]
                op(V.tensor_tensor_scan, deg, same[:, :], real[:, :], 0.0, ALU.mult, ALU.add)
                op(V.tensor_copy, side_s[:, 16:17], weight_sum[:, EC:EC + 1])
                op(V.tensor_tensor, for_counts, deg, pick[:, :], ALU.mult)
                op(V.tensor_reduce, side_s[:, 17:18], for_counts, AX, ALU.add)
                op(V.tensor_scalar, deg, deg, 1.0, None, ALU.max)
                op(V.reciprocal, rdeg[:, :], deg)

            def beside(f, *a, **k):
                return f(*a, **k).then_inc(dve_step, n.up())

            def row_stats(xt, s):
                for t in range(K):
                    beside(V.bn_stats, stats[:, s, t, :], xt[:, t, :])

            def moments(s):
                mean_a, sq_a, mean_b, sq_b = (stats[:, s, :, k] for k in (1, 2, 4, 5))
                op(V.tensor_tensor, rowsum[:, s, :], mean_a, mean_b, ALU.add)
                beside(V.tensor_tensor, apart[:, s, :], mean_a, mean_b, ALU.subtract)
                beside(V.tensor_tensor, sumsq[:, s, :], sq_a, sq_b, ALU.add)
                op(V.tensor_scalar, negmean[:, s, :], rowsum[:, s, :], -0.5, None, ALU.mult)
                beside(V.scalar_tensor_tensor, out=apart[:, s, :], in0=apart[:, s, :], scalar=D / 4.0,
                       in1=apart[:, s, :], op0=ALU.mult, op1=ALU.mult)
                settle()
                V.tensor_tensor(sumsq[:, s, :], sumsq[:, s, :], apart[:, s, :], ALU.add).then_inc(summed, 1)

            def center_rows(xt, s):
                op(V.tensor_tensor, tk(center[:, s, :]), xt, bc_f(negmean[:, s, :]), ALU.add)

            def scale_of(m, s):
                dve.wait_ge(deviated, m)
                op(V.reciprocal, rstd[:, s, :], std[:, s, :])

            def pick_side(pick, i, s, source, into):
                op(V.tensor_tensor, picked[:, :, :], source, bc_t(pick[:, cols(i, s)]), ALU.mult)
                op(V.tensor_reduce, side_part[:, :], picked[:, :, :], AX, ALU.add)
                op(V.tensor_tensor, into, into, side_part[:, :], ALU.add)

            def edge_back(layer, i, s, slot, norm, same_at, weights, pick):
                scale_of(norm, slot)
                op(V.tensor_tensor, coef[:, s, :], rstd[:, slot, :], weights[:, cols(i, s)], ALU.mult)
                to = by_slot(msg[:, s, :, 1:K + 1])
                h = tk(hrow[:, s, :]) if layer == 1 else to
                op(V.scalar_tensor_tensor, out=h, in0=tk(center[:, s, :]), scalar=0.0,
                   in1=bc_f(coef[:, s, :]), op0=ALU.max, op1=ALU.mult)
                if layer == 1:
                    op(V.tensor_tensor, to, h, tk(kept[:, fcols(i, s)]), ALU.mult)
                op(V.tensor_copy, msg[:, s, :, 0:1], run[:, 1 - s, :, K:K + 1])
                dve.wait_ge(mask_made, i * 2 + (same_at + s + 1))
                dve.wait_ge(sums_kept, i * 2 + (min(layer, 2) * CHUNKS + s + 1))
                settle()
                V.tensor_tensor_scan(flat(run[:, s, :, :]), flat(mask_rep[:, s, :, :]), flat(msg[:, s, :, :]),
                                     0.0, ALU.mult, ALU.add).then_inc(scanned, 1)
                dve.wait_ge(scanned, i * 2 + (same_at + s + 3))
                if pick is not None:
                    pick_side(pick, i, s, run[:, s, :, 1:K + 1], side_sum[:, :])

            for layer, pick, weights, cont, side_final in ((0, pick_d, wt, cont_d, side_final_d),
                                                           (1, pick_s, real, cont_s, side_final_s)):
                turn_masks(cont, 3 + 3 * layer)

                def front(i, s):
                    if layer == 0:
                        dve.wait_ge(got_free, i * 2 + (s + 3))
                        rows = tk(kept[:, fcols(i, s)])
                        row_stats(rows, s)
                        moments(s)
                        center_rows(rows, s)
                    else:
                        dve.wait_ge(landed[s], i * (16 * K) + (2 * LANDS + 16 * K))
                        rows = tk(got[:, s, 0:K * D])
                        row_stats(rows, s)
                        moments(s)
                        center_rows(rows, s)
                        settle()
                        dve.sem_inc(got_free, 1)

                def back(i, s):
                    edge_back(layer, i, s, s, i * 2 + (NORMS[layer] + s + 1), layer * CHUNKS, weights, pick)

                if layer == 1:
                    dve.wait_ge(got_free, 2 + 2 * CHUNKS)
                front(0, 0)
                with dve.Fori(0, PAIRS - 1) as i:
                    n.enter(i, 0, 54 if layer == 0 else 56)
                    front(i, 1)
                    back(i, 0)
                    front(i + 1, 0)
                    back(i, 1)
                    n.leave(PAIRS - 1)
                front(PAIRS - 1, 1)
                back(PAIRS - 1, 0)
                back(PAIRS - 1, 1)
                carry_sums(4 + 3 * layer, run[:, 1, :, K])
                if layer:
                    dve.wait_ge(side_scattered, 16 * layer)
                settle()
                V.tensor_tensor(side_out[:, :], side_sum[:, :], side_ps[:, 0:D], ALU.add).then_inc(side_made, 1)
                dve.wait_ge(side_made, layer + 1)
                op(V.memset, side_sum[:, :], 0.0)
                dve.wait_ge(sums_kept, (layer + 1) * CHUNKS + 2)
                op(V.memset, run[:, :, :, :], 0.0)

            turn_masks(cont_d, 9)
            op(V.tensor_scalar, d, same_d[:, :], BIG, -BIG, ALU.mult, ALU.add)
            op(V.tensor_scalar, cap[:, :], same_d[:, :], BIG, None, ALU.mult)
            op(V.tensor_tensor, cap[:, :], cap[:, :], d, ALU.add)
            degrees(same_d, pick_d)
            op(V.memset, score_max[:, 0:1], 0.0)
            op(V.memset, mask_rep[:, 0, :, :], 0.0)
            op(V.memset, mask_rep[:, 1, :, :], -BIG)
            settle()
            dve.sem_inc(masks_set, 1)

            def fronts(g, s):
                rows = tk(got[:, s, 0:K * D]), tk(got_dst[:, s, :])
                dve.wait_ge(landed[s], lands(g, s, 3 * LANDS))
                row_stats(rows[0], 0)
                dve.wait_ge(landed_dst[s], lands(g, s, 0))
                row_stats(rows[1], 1)
                moments(slice(0, 2))
                center_rows(rows[0], 0)
                center_rows(rows[1], 1)
                settle()
                dve.sem_inc(got_free, 1)
                dve.sem_inc(got_dst_free, 1)

            def lands(g, s, before):
                return (g - s) * (8 * K) + (16 * K + before)

            def backs(g, wait_turned=True):
                scale_of(g + (NORMS[2] + 1), slice(0, 2))
                for s in range(2):
                    if wait_turned:
                        dve.wait_ge(turned, g * 8 - 4 + 4 * s)
                    settle()
                    V.scalar_tensor_tensor(out=tk(hrow[:, s, :]), in0=tk(center[:, s, :]), scalar=0.0,
                                           in1=bc_f(rstd[:, s, :]), op0=ALU.max,
                                           op1=ALU.mult).then_inc(hrow_made, 1)

            def scores(i, s, last=False):
                dve.wait_ge(shares_made, i * 2 + (s + 1))
                c = cols(i, s)
                before = bass.ds(i * (2 * K) + s * K, 1)
                prev = bass.ds(i * (2 * K) + s * K, K)
                now = bass.ds(i * (2 * K) + s * K + 1, K)
                sh = share_ps[:, 0:2 * K].rearrange("p (t c) -> p t c", c=2)
                shd = share_ps[:, 2 * K:4 * K].rearrange("p (t c) -> p t c", c=2)
                op(V.tensor_tensor, score[:, :], sh[:, :, 0], w1t[:, c], ALU.mult)
                op(V.tensor_tensor, share[:, :], sh[:, :, 1], w1t[:, c], ALU.mult)
                op(V.tensor_tensor, score[:, :], score[:, :], shd[:, :, 0], ALU.add)
                op(V.tensor_copy, gate_dst[:, s, :], shd[:, :, 1])
                settle()
                dve.sem_inc(shares_used, 1)
                op(V.scalar_tensor_tensor, out=score[:, :], in0=score[:, :], scalar=0.01,
                   in1=score[:, :], op0=ALU.mult, op1=ALU.max)
                if last:
                    op(V.tensor_tensor, share[:, :], share[:, :], real[:, c], ALU.mult)
                    op(V.tensor_tensor, score[:, :], score[:, :], real[:, c], ALU.mult)
                    op(V.tensor_scalar, rowsum[:, 0, :], real[:, c], -LOW, LOW, ALU.mult, ALU.add)
                    op(V.tensor_tensor, score[:, :], score[:, :], rowsum[:, 0, :], ALU.add)
                op(V.tensor_tensor_scan, gate_sum[:, now], same_d[:, c], share[:, :],
                   gate_sum[:, before], ALU.mult, ALU.add)
                op(V.tensor_tensor_scan, score_max[:, now], cap[:, c], score[:, :],
                   score_max[:, before], ALU.min, ALU.max)
                op(V.tensor_tensor, expo[:, 0, :], score_max[:, prev], score_max[:, now], ALU.subtract)
                op(V.tensor_scalar, expo[:, 0, :], expo[:, 0, :], 0.0, None, ALU.min)
                settle()
                V.tensor_tensor(expo[:, 1, :], score[:, :], score_max[:, now],
                                ALU.subtract).then_inc(expo_made, 1)
                dve.wait_ge(exp_done, i * 2 + (s + 1))
                V.tensor_tensor(decay[:, s, :], wexp[:, s, 0, :], same_d[:, c], ALU.mult).then_inc(decay_made, 1)

            run_max = run[:, 1, :, :]
            run_sum = run[:, 0, :, :]

            def sums(i, s):
                c = cols(i, s)
                before = bass.ds(i * (2 * K) + s * K, 1)
                now = bass.ds(i * (2 * K) + s * K + 1, K)
                g1 = i * 2 + (s + 1)
                dve.wait_ge(decay_made, g1)
                op(V.tensor_tensor_scan, weight_sum[:, now], decay[:, s, :], wexp[:, s, 1, :],
                   weight_sum[:, before], ALU.mult, ALU.add)
                dve.wait_ge(proj_made, g1)
                op(V.tensor_tensor, by_slot(msg[:, 0, :, 1:K + 1]), tk(value_ps[:, 0:K * D]),
                   bc_f(wexp[:, s, 1, :]), ALU.mult)
                op(V.tensor_copy, msg[:, 0, :, 0:1], run_sum[:, :, K:K + 1])
                settle()
                dve.sem_inc(value_free, 1)
                dve.wait_ge(decay_rep, g1)
                V.tensor_tensor_scan(flat(run_sum), flat(mask_rep[:, 0, :, :]), flat(msg[:, 0, :, :]),
                                     0.0, ALU.mult, ALU.add).then_inc(scanned, 1)
                op(V.tensor_tensor, by_slot(msg[:, 1, :, 1:K + 1]), tk(feat_ps[:, 0:K * D]),
                   bc_f(w1t[:, c]), ALU.mult)
                op(V.tensor_copy, msg[:, 1, :, 0:1], run_max[:, :, K:K + 1])
                dve.wait_ge(mask_made, g1 + 2 * CHUNKS)
                settle()
                dve.sem_inc(feat_free, 1)
                V.tensor_tensor_scan(flat(run_max), flat(mask_rep[:, 1, :, :]), flat(msg[:, 1, :, :]),
                                     0.0, ALU.min, ALU.max).then_inc(gate_scanned, 1)
                dve.wait_ge(gate_scanned, g1 + 1)
                op(V.tensor_tensor, by_slot(picked[:, :, :]), by_slot(run_max[:, :, 1:K + 1]),
                   gmax_w[:, :].unsqueeze(1).to_broadcast([P, K, D]), ALU.mult)
                op(V.tensor_reduce, gate[:, :], by_slot(picked[:, :, :]), AX, ALU.add)
                op(V.tensor_tensor, coef[:, s, :], gate_sum[:, now], rdeg[:, c], ALU.mult)
                op(V.tensor_tensor, coef[:, s, :], coef[:, s, :], gate_dst[:, s, :], ALU.add)
                settle()
                V.tensor_tensor(gate[:, :], gate[:, :], coef[:, s, :], ALU.add).then_inc(gate_made, 1)
                dve.wait_ge(scanned, g1 + (2 * CHUNKS + 2))
                pick_side(pick_d, i, s, run_sum[:, :, 1:K + 1], side_sum[:, :])
                pick_side(pick_d, i, s, run_max[:, :, 1:K + 1], side_max[:, :])
                dve.wait_ge(gate_exp, g1)
                op(V.tensor_scalar, coef[:, s, :], weight_sum[:, now], 1e-30, None, ALU.max)
                op(V.scalar_tensor_tensor, out=coef[:, s, :], in0=gexp[:, :], scalar=1.0,
                   in1=coef[:, s, :], op0=ALU.add, op1=ALU.mult)
                op(V.reciprocal, rowsum[:, 0, :], coef[:, s, :])
                settle()
                V.tensor_tensor(tk(kept[:, fcols(i, s)]), by_slot(run_sum[:, :, 1:K + 1]),
                                bc_f(rowsum[:, 0, :]), ALU.mult).then_inc(kept_made, 1)
                dve.wait_ge(kept_made, g1)

            def attend(i, s, more=True, more2=True):
                g = i * 2 + s
                ni, ns = (i, 1) if s == 0 else (i + 1, 0)
                if more:
                    backs(g + 1)
                if more2:
                    fronts(g + 2, s)
                sums(i, s)
                if more:
                    scores(ni, ns, last=not more2)

            fronts(0, 0)
            backs(0, wait_turned=False)
            fronts(1, 1)
            scores(0, 0)
            op(V.tensor_copy, side_s[:, 6:7], gate_dst[:, 0, 0:1])
            with dve.Fori(0, PAIRS - 1) as i:
                n.enter(i, 0, 126)
                for s in range(2):
                    attend(i, s)
                n.leave(PAIRS - 1)
            attend(PAIRS - 1, 0, more2=False)
            attend(PAIRS - 1, 1, more=False, more2=False)

            op(V.tensor_copy, tails[:, 0, 0:D], run_sum[:, :, K])
            op(V.tensor_copy, tails[:, 0, D:W], weight_sum[:, EC:EC + 1])
            op(V.memset, tails[:, 1, :], 0.0)
            op(V.tensor_copy, tails[:, 1, 0:D], run_max[:, :, K])
            op(V.memset, tails[:, 2, :], 0.0)
            op(V.tensor_copy, tails[:, 2, 0:1], gate_sum[:, EC:EC + 1])
            op(V.tensor_copy, tails[:, 2, 1:2], side_s[:, 16:17])
            op(V.tensor_copy, tails[:, 3, :], score_max[:, EC:EC + 1].to_broadcast([P, W]))
            settle()
            dve.sem_inc(side_ready, 1)
            op(V.tensor_scalar, capT[:, :], maskT[:, 0, :], BIG, None, ALU.mult)
            op(V.tensor_scalar, maskT[:, 2, :], maskT[:, 0, :], BIG, -BIG, ALU.mult, ALU.add)
            op(V.tensor_tensor, capT[:, :], capT[:, :], maskT[:, 2, :], ALU.add)
            op(V.tensor_scalar, maskT[:, 2, :], maskT[:, 1, :], BIG, None, ALU.mult)
            op(V.tensor_scalar, expT[:, 0, :], maskT[:, 1, :], BIG, -BIG, ALU.mult, ALU.add)
            op(V.tensor_tensor, maskT[:, 2, :], maskT[:, 2, :], expT[:, 0, :], ALU.add)
            op(V.memset, chainT[:, :, 0:1], 0.0)
            for k, array in enumerate((score_max, gate_sum, weight_sum)):
                op(V.tensor_tensor, for_counts, array[:, 1:1 + EC], pick_d[:, :], ALU.mult)
                op(V.tensor_reduce, side_s[:, 18 + k:19 + k], for_counts, AX, ALU.add)
            dve.wait_ge(side_turned, 10)

            def ps(c):
                return side_ps[0:W, c * P:(c + 1) * P]

            op(V.tensor_tensor_scan, chainT[:, 3, 1:P + 1], capT[:, :], ps(3), 0.0, ALU.min, ALU.max)
            op(V.tensor_tensor, expT[:, 0, :], chainT[:, 3, 0:P], chainT[:, 3, 1:P + 1], ALU.subtract)
            op(V.tensor_scalar, expT[:, 0, :], expT[:, 0, :], 0.0, None, ALU.min)
            settle()
            V.tensor_tensor(expT[:, 1, :], ps(3), chainT[:, 3, 1:P + 1], ALU.subtract).then_inc(side_act, 1)
            dve.wait_ge(side_acted, 1)
            op(V.tensor_tensor, wexpT[:, 0, :], wexpT[:, 0, :], maskT[:, 0, :], ALU.mult)
            op(V.tensor_tensor, wexpT[:, 1, :], wexpT[:, 1, :], ps(0), ALU.mult)
            op(V.tensor_tensor_scan, chainT[:, 0, 1:P + 1], wexpT[:, 0, :], wexpT[:, 1, :], 0.0, ALU.mult, ALU.add)
            op(V.tensor_tensor_scan, chainT[:, 1, 1:P + 1], capT[:, :], ps(1), 0.0, ALU.min, ALU.max)
            op(V.tensor_tensor_scan, chainT[:, 2, 1:P + 1], maskT[:, 0, :], ps(2), 0.0, ALU.mult, ALU.add)
            op(V.tensor_tensor, inT[:, 0, :], chainT[:, 0, 0:P], maskT[:, 1, :], ALU.mult)
            op(V.tensor_tensor, inT[:, 1, :], chainT[:, 1, 0:P], maskT[:, 2, :], ALU.min)
            op(V.tensor_tensor, inT[:, 2, :], chainT[:, 2, 0:P], maskT[:, 1, :], ALU.mult)
            op(V.tensor_tensor, inT[:, 3, :], chainT[:, 3, 0:P], maskT[:, 2, :], ALU.min)
            op(V.tensor_scalar, inT[:, 3, :], inT[:, 3, :], LOW, None, ALU.max)
            settle()
            dve.sem_inc(side_ready, 1)
            dve.wait_ge(side_turned, 11)

            def back_ps(c, a, b):
                return side_ps[:, c * P + a:c * P + b]

            op(V.tensor_tensor, side_s[:, 7:8], side_s[:, 18:19], back_ps(3, 0, 1), ALU.max)
            op(V.tensor_tensor, side_s[:, 8:9], side_s[:, 18:19], side_s[:, 7:8], ALU.subtract)
            settle()
            V.tensor_tensor(side_s[:, 9:10], back_ps(3, 0, 1), side_s[:, 7:8], ALU.subtract).then_inc(side_act, 1)
            dve.wait_ge(side_acted, 2)
            op(V.tensor_scalar, side_part[:, :], back_ps(0, 0, D), side_s[:, 11:12], None, ALU.mult)
            op(V.scalar_tensor_tensor, out=side_sum[:, :], in0=side_sum[:, :], scalar=side_s[:, 10:11],
               in1=side_part[:, :], op0=ALU.mult, op1=ALU.add)
            op(V.tensor_scalar, side_s[:, 12:13], back_ps(0, D, W), side_s[:, 11:12], None, ALU.mult)
            op(V.scalar_tensor_tensor, out=side_s[:, 12:13], in0=side_s[:, 20:21], scalar=side_s[:, 10:11],
               in1=side_s[:, 12:13], op0=ALU.mult, op1=ALU.add)
            op(V.tensor_scalar, side_s[:, 12:13], side_s[:, 12:13], 1e-30, None, ALU.max)
            op(V.tensor_tensor, side_max[:, :], side_max[:, :], back_ps(1, 0, D), ALU.max)
            op(V.tensor_tensor, side_part[:, :], side_max[:, :], gmax_w[:, :], ALU.mult)
            op(V.tensor_reduce, side_s[:, 13:14], side_part[:, :], AX, ALU.add)
            op(V.tensor_tensor, side_s[:, 21:22], side_s[:, 19:20], back_ps(2, 0, 1), ALU.add)
            op(V.tensor_tensor, side_s[:, 22:23], side_s[:, 17:18], back_ps(2, 1, 2), ALU.add)
            op(V.tensor_scalar, side_s[:, 22:23], side_s[:, 22:23], 1.0, None, ALU.max)
            op(V.reciprocal, side_s[:, 23:24], side_s[:, 22:23])
            op(V.scalar_tensor_tensor, out=side_s[:, 21:22], in0=side_s[:, 21:22], scalar=side_s[:, 23:24],
               in1=side_s[:, 13:14], op0=ALU.mult, op1=ALU.add)
            settle()
            V.tensor_tensor(side_s[:, 14:15], side_s[:, 21:22], side_s[:, 6:7], ALU.add).then_inc(side_act, 1)
            dve.wait_ge(side_acted, 3)
            op(V.scalar_tensor_tensor, out=side_s[:, 12:13], in0=side_s[:, 15:16], scalar=1.0,
               in1=side_s[:, 12:13], op0=ALU.add, op1=ALU.mult)
            op(V.reciprocal, side_s[:, 13:14], side_s[:, 12:13])
            dve.wait_ge(side_scattered, 32)
            settle()
            V.tensor_scalar(side_out[:, :], side_sum[:, :], side_s[:, 13:14], None, ALU.mult).then_inc(side_made, 1)

            dve.wait_ge(side_made, 3)

            op(V.memset, side_sum[:, :], 0.0)
            op(V.memset, run[:, :, :, :], 0.0)
            op(V.memset, mask_rep[:, :, :, :], 0.0)
            turn_masks(cont_s, 12)
            degrees(same_s, pick_s)
            settle()
            dve.sem_inc(masks_set, 1)

            def edge_front(i, s, g):
                rows = tk(got[:, s, 0:K * D])
                dve.wait_ge(landed[s], i * (16 * K) + (4 * LANDS + 16 * K))
                op(V.tensor_reduce, rowsum[:, 2 + s, :], rows, AX, ALU.add)
                op(V.tensor_scalar, negmean[:, 2 + s, :], rowsum[:, 2 + s, :], -1.0 / D, None, ALU.mult)
                settle()
                V.tensor_tensor(tk(center[:, s, :]), rows, bc_f(negmean[:, 2 + s, :]),
                                ALU.add).then_inc(centered, 1)
                dve.wait_ge(centered, g + 1)
                dve.sem_inc(got_free, 1)

            def edge_squares(s, g):
                dve.wait_ge(squared, g + 1)
                V.tensor_reduce(sumsq[:, 2 + s, :], tk(square[:, s, :]), AX, ALU.add).then_inc(summed, 1)

            def tile(j):
                return rowin[:, j * K * D:(j + 1) * K * D]

            def tile_front(i, j):
                dve.wait_ge(x_loaded[j], i * 32 + 32)
                row_stats(tk(tile(j)), j % 2)

            def tiles_back(i, s):
                scale_of(i * 4 + (NORMS[3] + 2 * s + 1), slice(0, 2))
                settle()
                V.tensor_tensor(shift[:, :, :], negmean[:, 0:2, :], rstd[:, 0:2, :], ALU.mult).then_inc(shifted, 1)

            def add_rows(i, j, start=False):
                if not start:
                    dve.wait_ge(outs_stored[j % 2], i * 64 + 32 * (j // 2))
                dve.wait_ge(rows_made, i * 4 + (j + 1))
                V.tensor_tensor(outrow[:, j % 2, :], tile(j), hrow[:, j % 2, :], ALU.add).then_inc(out_made, 1)
                dve.wait_ge(out_made, i * 4 + (j + 1))
                dve.sem_inc(x_used, 1)

            def half(i, s, start=False, last=False):
                g = i * 2 + s
                ni, ns = i + s, 1 - s
                if not last:
                    tile_front(ni, 2 * ns)
                edge_back(3, i, s, 2 + s, i * 4 + (NORMS[3] + 2 * s + 2), 3 * CHUNKS, real, None)
                if not last:
                    tile_front(ni, 2 * ns + 1)
                    moments(slice(0, 2))
                add_rows(i, 2 * s, start)
                before_last = isinstance(i, int) and i == PAIRS - 1 and s == 0
                if not last and not before_last:
                    edge_front(ni, ns, g + 1)
                add_rows(i, 2 * s + 1, start)
                if before_last:
                    tiles_back(ni, ns)
                    edge_front(ni, ns, g + 1)
                if not last:
                    edge_squares(ns, g + 1)
                if not last and not before_last:
                    tiles_back(ni, ns)

            for j in range(2):
                tile_front(0, j)
            moments(slice(0, 2))
            tiles_back(0, 0)
            edge_front(0, 0, 0)
            edge_squares(0, 0)
            half(0, 0, start=True)
            half(0, 1)
            with dve.Fori(1, PAIRS - 1) as i:
                n.enter(i, 1, 80)
                for s in range(2):
                    half(i, s)
                n.leave(PAIRS - 2)
            half(PAIRS - 1, 0)
            half(PAIRS - 1, 1, last=True)
            for s in range(2):
                dve.wait_ge(outs_stored[s], 16 * TILES)

            def means(i, s):
                c = tk(kept[:, fcols(i, s)])
                dve.wait_ge(sums_kept, i * 2 + (2 * CHUNKS + s + 3))
                dve.wait_ge(outrow_free, i * 2 + (3 * CHUNKS + s + 1))
                V.tensor_copy(stage_out[:, s, :], final_s[:, cols(i, s)]).then_inc(out_staged, 1)
                V.tensor_tensor(tk(outrow[:, s, :]), c, bc_f(rdeg[:, cols(i, s)]), ALU.mult).then_inc(outrow_made, 1)
                pick_side(pick_s, i, s, by_feature(c), side_sum[:, :])

            with dve.Fori(0, PAIRS) as i:
                n.enter(i, 0, 6)
                for s in range(2):
                    means(i, s)
                n.leave(PAIRS)
            carry_sums(13, run[:, 1, :, K], side_s[:, 16:17])
            op(V.tensor_tensor, side_s[:, 0:1], side_s[:, 17:18], side_ps[:, P:P + 1], ALU.add)
            op(V.tensor_scalar, side_s[:, 0:1], side_s[:, 0:1], 1.0, None, ALU.max)
            op(V.reciprocal, side_s[:, 1:2], side_s[:, 0:1])
            op(V.tensor_tensor, side_sum[:, :], side_sum[:, :], side_ps[:, 0:D], ALU.add)
            dve.wait_ge(side_scattered, 48)
            settle()
            V.tensor_scalar(side_out[:, :], side_sum[:, :], side_s[:, 1:2], None, ALU.mult).then_inc(side_made, 1)


def kernel(x, src, dst, edge_attr_64, edge_weight, edge_weight1, L2_gnn_Wa, L2_gnn_att_w, L2_gnn_Wg,
           L2_gnn_gate_w):
    import numpy as np
    import concourse.bacc as bacc
    from concourse.bass_utils import run_bass_kernel_spmd

    arrays = {
        "x_in": x, "src_in": np.reshape(src, (-1, 1)), "dst_in": np.reshape(dst, (-1, 1)),
        "attr_in": edge_attr_64, "w_in": np.reshape(edge_weight, (-1, 1)), "w1_in": edge_weight1,
        "Wa_in": L2_gnn_Wa, "att_in": L2_gnn_att_w, "Wg_in": L2_gnn_Wg, "gate_in": L2_gnn_gate_w,
    }
    arrays = {name: np.ascontiguousarray(a) for name, a in arrays.items()}
    N = arrays["x_in"].shape[0]
    nc = bacc.Bacc("TRN2", target_bir_lowering=False, num_devices=1)
    ins = [nc.dram_tensor(name, a.shape, mybir.dt.from_np(a.dtype), kind="ExternalInput").ap()
           for name, a in arrays.items()]
    out = nc.dram_tensor("x_out", (N + (2 * K + 1) * P, D), F32, kind="ExternalOutput").ap()
    gnn_kernel(nc, *ins, out)
    result = run_bass_kernel_spmd(nc, [arrays], core_ids=[0])
    return result.results[0]["x_out"][:N]
```
